# Optimizing a Trainium2 kernel written in Bass

```python
import numpy as np
import jax
import jax.numpy as jnp

def _softmax(x, axis=-1):
    return jax.nn.softmax(x, axis=axis)

def _gelu(x):
    return jax.nn.gelu(x, approximate=True)

def _silu(x):
    return jax.nn.silu(x)

def _sigmoid(x):
    return jax.nn.sigmoid(x)

def _layernorm(x, axis=-1, eps=1e-05):
    m = jnp.mean(x, axis=axis, keepdims=True)
    v = jnp.var(x, axis=axis, keepdims=True)
    return (x - m) / jnp.sqrt(v + eps)

def _scatter_add(tgt, idx, src, axis=0):
    return tgt.at[idx].add(src)

def _segment_sum(src, seg, n):
    return jax.ops.segment_sum(src, seg, n)
kernel_name = 'mk_flamingo_gated_d1_seqx_r4_fb8cf6'

def setup_inputs(seed: int=0):
    np.random.seed(seed)
    _w = jnp.asarray

    def _rec_inputs():
        import jax
        import jax.numpy as jnp
        _rk = jax.random.key(seed)
        x = 0.0003765 + 1 * jax.random.normal(jax.random.fold_in(_rk, 1), (16, 256, 512), jnp.float32)
        _lenS = 256 - jax.random.randint(jax.random.fold_in(_rk, 7), (16,), 0, max(1, 256 // 4) + 1, jnp.int32)
        _lenS2 = 256 - jax.random.randint(jax.random.fold_in(_rk, 8), (16,), 0, max(1, 256 // 4) + 1, jnp.int32)
        _ctx_2048P = jax.random.normal(jax.random.fold_in(_rk, 11), (16, 16, 512), jnp.float32)
        _ctx_2048c = jax.random.dirichlet(jax.random.fold_in(_rk, 511), 0.3 * jnp.ones((16,), jnp.float32), (16, 256))
        _ctx_2048t = jnp.einsum('bsk,bkd->bsd', _ctx_2048c, _ctx_2048P)
        _ctx_2048t = _ctx_2048t * jax.lax.rsqrt(jnp.mean(jnp.square(_ctx_2048t)) + 1e-12) * 0.953939
        ctx_2048 = -0.000292821 + 1.00034 * (_ctx_2048t + 0.3 * jax.random.normal(jax.random.fold_in(_rk, 611), (16, 256, 512), jnp.float32))
        _g = jax.random.normal(jax.random.fold_in(_rk, 9001), (2, 1), jnp.float32)
        _g = jnp.sign(_g) * jnp.maximum(jnp.abs(_g), 1.0) + (_g == 0) * 1.0
        g_xattn = _g[0]
        g_ffn = _g[1]
        return (x, ctx_2048, g_xattn, g_ffn)
    x, ctx_2048, g_xattn, g_ffn = _rec_inputs()

    def _L0_xattn_setup():
        import jax, jax.numpy as jnp
        import numpy as np
        key = jax.random.key(seed)
        k1, k2, k3, k4, k5 = jax.random.split(key, 5)
        B, D_MODEL, L = (2, 256, 512)
        HEAD_DIM = 8
        H = D_MODEL // HEAD_DIM
        return {'k': jax.random.normal(k1, (B, D_MODEL, L), dtype=jnp.float32), 'v': jax.random.normal(k2, (B, D_MODEL, L), dtype=jnp.float32), 'q': jax.random.normal(k3, (B, D_MODEL, L), dtype=jnp.float32), 'ssm_kernel': jax.random.normal(k4, (H, L), dtype=jnp.float32), 'D': jax.random.normal(k5, (H,), dtype=jnp.float32), 'head_dim': HEAD_DIM}
    _L0_xattn_all = _L0_xattn_setup()
    _L0_xattn_in = {k: v for k, v in _L0_xattn_all.items() if k in ('ssm_kernel', 'D')}
    del _L0_xattn_all

    def _L0_ffn_setup():
        import jax, jax.numpy as jnp
        import numpy as np
        L, B, D = (512, 1, 512)
        H = 16
        DK, DV = (D // 2, D)
        HDK, HDV = (DK // H, DV // H)
        RATIO = 2
        BASE = 10000.0
        EPS = 1e-05

        def _apply_rotary(x, cos, sin):
            d2 = x.shape[-1] // 2
            x1, x2 = (x[..., :d2], x[..., d2:])
            return jnp.concatenate([x1 * cos - x2 * sin, x2 * cos + x1 * sin], axis=-1)
        key = jax.random.key(seed)
        ks = jax.random.split(key, 8)
        s = 0.02
        return {'x': jax.random.normal(ks[0], (L, B, D), jnp.float32), 'conv_w': jax.random.normal(ks[1], (D, 2), jnp.float32) * 0.5, 'Wq': jax.random.normal(ks[2], (D, DK), jnp.float32) * s, 'Wk': jax.random.normal(ks[3], (D, DK), jnp.float32) * s, 'Wv': jax.random.normal(ks[4], (D, DV), jnp.float32) * s, 'Wg': jax.random.normal(ks[5], (D, DV), jnp.float32) * s, 'router_w': jax.random.normal(ks[6], (H, HDV, RATIO), jnp.float32) * s, 'Wout': jax.random.normal(ks[7], (DV, D), jnp.float32) * s}
    _L0_ffn_all = _L0_ffn_setup()
    _L0_ffn_in = {k: v for k, v in _L0_ffn_all.items() if k in ('conv_w', 'Wq', 'Wk', 'Wv', 'Wg', 'router_w', 'Wout')}
    del _L0_ffn_all
    return {'x': x, 'ctx_2048': ctx_2048, 'g_xattn': g_xattn, 'g_ffn': g_ffn, 'L0_xattn_ssm_kernel': _L0_xattn_in['ssm_kernel'], 'L0_xattn_D': _L0_xattn_in['D'], 'L0_ffn_conv_w': _L0_ffn_in['conv_w'], 'L0_ffn_Wq': _L0_ffn_in['Wq'], 'L0_ffn_Wk': _L0_ffn_in['Wk'], 'L0_ffn_Wv': _L0_ffn_in['Wv'], 'L0_ffn_Wg': _L0_ffn_in['Wg'], 'L0_ffn_router_w': _L0_ffn_in['router_w'], 'L0_ffn_Wout': _L0_ffn_in['Wout']}

def reference(x, ctx_2048, g_xattn, g_ffn, L0_xattn_ssm_kernel, L0_xattn_D, L0_ffn_conv_w, L0_ffn_Wq, L0_ffn_Wk, L0_ffn_Wv, L0_ffn_Wg, L0_ffn_router_w, L0_ffn_Wout):
    import jax
    import jax.numpy as jnp

    def _L0_xattn_ref(k, v, q, ssm_kernel, D, head_dim):
        import jax, jax.numpy as jnp
        import numpy as np
        B, HD, L = k.shape
        H = HD // head_dim
        fft_size = 2 * L
        k_ = k.reshape(B, H, head_dim, L)
        v_ = v.reshape(B, H, head_dim, L)
        q_ = q.reshape(B, H, head_dim, L)
        kv = jnp.einsum('bhil,bhjl->bijhl', k_, v_)
        kv_f = jnp.fft.rfft(kv, n=fft_size)
        kernel_f = jnp.fft.rfft(ssm_kernel, n=fft_size)
        y = jnp.fft.irfft(kv_f * kernel_f, n=fft_size)[..., :L]
        out = y + kv * D[None, None, None, :, None]
        out = jnp.einsum('bijhl,bhil->bjhl', out, q_)
        out = jnp.transpose(out, (0, 2, 1, 3)).reshape(B, H * head_dim, L)
        return out.astype(k.dtype)

    def _L0_ffn_ref(x, conv_w, Wq, Wk, Wv, Wg, router_w, Wout):
        import jax, jax.numpy as jnp
        import numpy as np
        L, B, D = (512, 1, 512)
        H = 16
        DK, DV = (D // 2, D)
        HDK, HDV = (DK // H, DV // H)
        RATIO = 2
        BASE = 10000.0
        EPS = 1e-05

        def _apply_rotary(x, cos, sin):
            d2 = x.shape[-1] // 2
            x1, x2 = (x[..., :d2], x[..., d2:])
            return jnp.concatenate([x1 * cos - x2 * sin, x2 * cos + x1 * sin], axis=-1)
        x = jnp.transpose(x, (1, 0, 2))
        b, l, d = x.shape
        x_prev = jnp.pad(x, ((0, 0), (1, 0), (0, 0)))[:, :l]
        x = jax.nn.silu(x_prev * conv_w[:, 0] + x * conv_w[:, 1])
        q = jax.nn.silu(x @ Wq)
        k = x @ Wk
        v = x @ Wv
        g = x @ Wg
        q = q.reshape(b, l, H, HDK).transpose(0, 2, 1, 3)
        k = k.reshape(b, l, H, HDK).transpose(0, 2, 1, 3)
        v = v.reshape(b, l, H, HDV).transpose(0, 2, 1, 3)
        inv_freq = 1.0 / BASE ** (jnp.arange(0, HDK, 2, dtype=jnp.float32) / HDK)
        freqs = jnp.arange(l, dtype=jnp.float32)[:, None] * inv_freq[None, :]
        cos, sin = (jnp.cos(freqs), jnp.sin(freqs))
        q = _apply_rotary(q, cos, sin)
        k = _apply_rotary(k, cos, sin)
        logits = jnp.einsum('bhld,hdr->bhlr', v, router_w)
        scores = jax.nn.softmax(logits, axis=-1)
        onehot = jax.nn.one_hot(jnp.argmax(scores, axis=-1), RATIO, dtype=scores.dtype)
        masked_scores = scores * onehot
        masked_ind = onehot
        sum_ind = jnp.cumsum(masked_ind, axis=2)
        norm = jnp.where(sum_ind > 0, 1.0 / jnp.maximum(sum_ind, 1.0), 0.0)[..., None]
        q_exp = q[:, :, :, None, :] * masked_scores[..., None] * norm
        k_exp = k[:, :, :, None, :] * masked_ind[..., None]
        q_exp = q_exp.reshape(b, H, l, RATIO * HDK)
        k_exp = k_exp.reshape(b, H, l, RATIO * HDK)
        qk = jnp.einsum('bhld,bhmd->bhlm', q_exp, k_exp) * HDK ** (-0.5)
        mask = jnp.tril(jnp.ones((l, l), dtype=qk.dtype))
        qk = qk * mask
        o = jnp.einsum('bhlm,bhmd->bhld', qk, v)
        o = o.transpose(0, 2, 1, 3)
        mu = jnp.mean(o, axis=-1, keepdims=True)
        var = jnp.var(o, axis=-1, keepdims=True)
        o = (o - mu) / jnp.sqrt(var + EPS)
        out = jax.nn.silu(g) * o.reshape(b, l, d)
        out = out @ Wout
        return jnp.transpose(out, (1, 0, 2))
    x = x + jnp.tanh(g_xattn[0]) * _L0_xattn_ref(ctx_2048, ctx_2048, _layernorm(x, axis=-1), L0_xattn_ssm_kernel, L0_xattn_D, 8)
    x = x + jnp.tanh(g_ffn[0]) * _L0_ffn_ref(_layernorm(x, axis=-1), L0_ffn_conv_w, L0_ffn_Wq, L0_ffn_Wk, L0_ffn_Wv, L0_ffn_Wg, L0_ffn_router_w, L0_ffn_Wout)
    return x

_drawn_inputs = setup_inputs


def setup_inputs(seed=0):
    import zlib

    import numpy as np

    out = dict(_drawn_inputs(seed))
    spreads = {}
    factors = {'L0_ffn_conv_w': 8.0,
     'L0_ffn_Wq': 8.0,
     'L0_ffn_Wk': 8.0,
     'L0_ffn_Wv': 8.0,
     'L0_ffn_Wg': 8.0,
     'L0_ffn_router_w': 8.0,
     'L0_ffn_Wout': 8.0}
    for name, (base, spread) in spreads.items():
        noise = np.random.default_rng([zlib.crc32(name.encode()), seed]).standard_normal(out[name].shape)
        drawn = base * np.exp(spread * noise) if base else spread * noise
        out[name] = jnp.asarray(drawn.astype(out[name].dtype))
    for name, factor in factors.items():
        out[name] = (out[name] * factor).astype(out[name].dtype)
    return out
```

```python
from contextlib import ExitStack

import numpy as np

import concourse.bass as bass
from concourse import mybir

ALU = mybir.AluOpType
ACT = mybir.ActivationFunctionType
F32 = mybir.dt.float32
AX_X = mybir.AxisListType.X

P = 128
EPS = 1e-5
C_ID, C_MASK, C_CAUSAL, C_COS, C_SIN, C_HALF, C_COLS = 0, 128, 256, 384, 400, 416, 417


def view(ap, dims):
    return bass.AP(tensor=ap.tensor, offset=ap.offset, ap=[ap.ap[0]] + dims)


def can_wait(value):
    return not isinstance(value, int) or value > 0


def flamingo_gated_layer(nc, x, ctx_in, g_xattn, g_ffn, ssm_kernel, ssm_D, conv_w, Wq, Wk, Wv, Wg,
                         router_w, Wout, consts, out):
    NB, ROWS, L = x.shape
    HD = NB // 2
    NH = ROWS // HD
    CH = L // P
    RH, HDV, RATIO = router_w.shape
    DK = Wq.shape[1]
    HDK = DK // RH
    DV = Wv.shape[1]
    NROT = HD // 2
    FULL = NROT * HD * NB
    HALF = HD // 2 * NB
    EXT = (HD + NROT) * NB
    ROW = HD * NB
    PROJ = 2 * DK + 2 * DV

    xg = x.rearrange("b (h j) l -> h j b l", j=HD)
    cg = ctx_in.rearrange("b (h j) l -> h j b l", j=HD)
    og = out.rearrange("b (h j) l -> h j b l", j=HD)
    taps_dram = nc.dram_tensor("taps_dram", (NH, P + L), F32, kind="Internal")

    with ExitStack() as stack:
        def sb(name, *free):
            return stack.enter_context(nc.sbuf_tensor(name, [P, *free], F32))

        def sem(name):
            return stack.enter_context(nc.semaphore(name))

        const = sb("const", C_COLS)
        w_all = sb("w_all", CH, PROJ)
        w_logit = sb("w_logit", CH, RH)
        w_out = sb("w_out", CH, L)
        w_conv = sb("w_conv", CH, 2)
        gates = sb("gates", 2)
        taps = sb("taps", P + L)
        d_tap = sb("d_tap", 1)
        router = sb("router", RH * HDV, RATIO)
        router_d = sb("router_d", RH * HDV)
        w_tmp = sb("w_tmp", CH, DV)
        w_mean = sb("w_mean", CH, RH)
        minus_half = sb("minus_half", RH)
        x_in = sb("x_in", 2, L)
        c_in = sb("c_in", 2, L)
        c_rev = sb("c_rev", CH, P)
        toep = sb("toep", 2, L)
        held = sb("held", 1)
        stats1 = sb("stats1", 6)
        mv1 = sb("mv1", 2)
        ve1 = sb("ve1", 1)
        rstd1 = sb("rstd1", 1)
        qn = sb("qn", L)
        kx = sb("kx", CH, EXT)
        qx = sb("qx", 2, CH, EXT)
        kv = sb("kv", 2, CH, FULL + HALF)
        z_terms = sb("z_terms", CH, 8 * ROW)
        x2 = sb("x2", 2, L)
        stats2 = sb("stats2", 6)
        mv2 = sb("mv2", 2)
        ve2 = sb("ve2", 1)
        rstd2 = sb("rstd2", 1)
        z = sb("z", L)
        y_raw = sb("y_raw", CH, P)
        yT = sb("yT", CH, P)
        qk_sb = sb("qk_sb", 2 * RH, HDK)
        rot_a = sb("rot_a", 2 * RH, HDK)
        rot_b = sb("rot_b", 2 * RH, HDK)
        rot = sb("rot", 2 * RH, HDK)
        v_sb = sb("v_sb", DV)
        gate_sb = sb("gate_sb", DV)
        d_log = sb("d_log", RH)
        u = sb("u", RH)
        th = sb("th", RH)
        score = sb("score", RH)
        score1 = sb("score1", RH)
        cnt_a = sb("cnt_a", RH)
        cnt = sb("cnt", RH)
        rcnt = sb("rcnt", RH)
        weight = sb("weight", RH)
        k_sel = sb("k_sel", RH, RATIO)
        q_sel = sb("q_sel", RH, RATIO)
        qe = sb("qe", RH, RATIO * HDK)
        ke = sb("ke", RH, RATIO * HDK)
        qeT = sb("qeT", CH, P)
        keT = sb("keT", CH, P)
        att = sb("att", CH, CH, P)
        o_sq = sb("o_sq", RH, HDV)
        o_var = sb("o_var", RH)
        o_ve = sb("o_ve", RH)
        o_rstd = sb("o_rstd", RH)
        o_n = sb("o_n", DV)
        gated = sb("gated", DV)
        gatedT = sb("gatedT", CH, P)
        out_sb = sb("out_sb", 2, L)

        bank = [stack.enter_context(nc.psum_tensor(f"bank{i}", [P, 512], F32)) for i in range(8)]

        ident = const[:, C_ID:C_ID + P]
        mask = const[:, C_MASK:C_MASK + P]
        causal = const[:, C_CAUSAL:C_CAUSAL + P]

        s_taps_in, s_taps_out, s_consts, s_weights, s_wout = (
            sem("s_taps_in"), sem("s_taps_out"), sem("s_consts"), sem("s_weights"), sem("s_wout"))
        s_x = [sem(f"s_x{i}") for i in range(2)]
        s_c = [sem(f"s_c{i}") for i in range(2)]
        s_toep = [sem(f"s_toep{i}") for i in range(2)]
        s_stored = [sem(f"s_stored{i}") for i in range(2)]
        taps_zero, taps_ready, gates_ready, wout_ready = (
            sem("taps_zero"), sem("taps_ready"), sem("gates_ready"), sem("wout_ready"))
        w_step, w_ready, half_ready, z_ready0 = sem("w_step"), sem("w_ready"), sem("half_ready"), sem("z_ready0")
        gatedT_ps, zT_ps, out_ps, logit_ps, qk_ps, v_ps, g_ps, cnt_ps = (
            sem(n) for n in ("gatedT_ps", "zT_ps", "out_ps", "logit_ps", "qk_ps", "v_ps", "g_ps", "cnt_ps"))
        conv_ps = [sem(f"conv_ps{i}") for i in range(CH)]
        qeT_ps, keT_ps, cT_ps, qT_ps, attn_ps, xo_ps, o_ps = (
            sem(n) for n in ("qeT_ps", "keT_ps", "cT_ps", "qT_ps", "attn_ps", "xo_ps", "o_ps"))
        gatedT_sb, y_cur, y_ready, th_ready, qk_copied, v_copied, gate_ready = (
            sem(n) for n in ("gatedT_sb", "y_cur", "y_ready", "th_ready", "qk_copied", "v_copied", "gate_ready"))
        qeT_sb, keT_sb, kx_ready, qx_ready, o_squared = (
            sem(n) for n in ("qeT_sb", "keT_sb", "kx_ready", "qx_ready", "o_squared"))
        crev_ready = sem("crev_ready")
        rot_prod, rot_ready, rstd1_ready, rstd2_ready, o_rstd_ready = (
            sem(n) for n in ("rot_prod", "rot_ready", "rstd1_ready", "rstd2_ready", "o_rstd_ready"))
        kv_ready = [sem(f"kv_ready{i}") for i in range(CH)]
        mul_done = [sem(f"mul_done{i}") for i in range(CH)]
        mask_done = [sem(f"mask_done{i}") for i in range(CH)]
        (mul_last, y_conv, out_ready, d_ready, u_ready, ksel_ready, route_a, route_b, route_c, qsel_ready,
         q1sel_ready, ke_ready, qe_ready, bn1_done, mv1_done, ve1_ready, qn_ready, x2_ready, bn2_done, mv2_done,
         ve2_ready, z_ready, o_summed, o_ve_ready, o_normed, gated_ready) = (
            sem(n) for n in ("mul_last", "y_conv", "out_ready", "d_ready", "u_ready", "ksel_ready", "route_a",
                             "route_b", "route_c", "qsel_ready", "q1sel_ready", "ke_ready", "qe_ready", "bn1_done",
                             "mv1_done", "ve1_ready", "qn_ready", "x2_ready", "bn2_done", "mv2_done", "ve2_ready",
                             "z_ready", "o_summed", "o_ve_ready", "o_normed", "gated_ready"))

        FIRST, LAST = -2, NH
        LOOP = (2, NH // 2 - 2)

        def run(eng, step):
            def peeled(h):
                step(h // 2, h % 2, 0 <= h - 1, 0 <= h < NH, 0 <= h + 1 < NH, h + 2 < NH)
            for h in range(FIRST, 2 * LOOP[0]):
                peeled(h)
            with eng.Fori(*LOOP) as t:
                for p in range(2):
                    step(t, p, True, True, True, True)
            for h in range(2 * LOOP[1], LAST + 1):
                peeled(h)

        block = stack.enter_context(nc.Block())

        @block.sync
        def _(eng):
            eng.dma_start(taps[0:NH, P:P + L], ssm_kernel).then_inc(s_taps_in, 16)
            eng.dma_start(d_tap[0:NH, :], ssm_D.rearrange("(h a) -> h a", a=1)).then_inc(s_taps_in, 16)
            eng.dma_start(const[:, :], consts).then_inc(s_consts, 16)
            eng.dma_start(c_in[:, 0, :], cg[0]).then_inc(s_c[0], 16)
            eng.dma_start(x_in[:, 0, :], xg[0]).then_inc(s_x[0], 16)
            eng.wait_ge(taps_ready, 1)
            eng.dma_start(taps_dram.ap(), taps[0:NH, :]).then_inc(s_taps_out, 16)
            eng.dma_start(c_in[:, 1, :], cg[1]).then_inc(s_c[1], 16)
            for w, c0, cols in ((Wv, 2 * DK, DV), (Wq, 0, DK), (Wk, DK, DK), (Wg, 2 * DK + DV, DV)):
                eng.dma_start(w_all[:, :, c0:c0 + cols], w.rearrange("(c p) n -> p c n", p=P)).then_inc(s_weights, 16)
            eng.dma_start(w_out[:, :, :], Wout.rearrange("(c p) n -> p c n", p=P)).then_inc(s_wout, 16)
            eng.wait_ge(s_taps_out, 16)

            def toeplitz(t, p, h):
                src = taps_dram.ap()[h, :]
                src = bass.AP(tensor=src.tensor, offset=src.offset + 1, ap=[[1, P], [1, L]])
                eng.dma_start(toep[:, p, :], src).then_inc(s_toep[p], 16)

            def step(t, p, tail, back, front, pre):
                h = 2 * t + p
                if pre:
                    if not (isinstance(h, int) and h < -1):
                        if can_wait(h + 1):
                            eng.wait_ge(x2_ready, h + 1)
                        eng.dma_start(x_in[:, p, :], xg[h + 2]).then_inc(s_x[p], 16)
                    if can_wait(h + 1):
                        eng.wait_ge(conv_ps[CH - 1], h + 1)
                    toeplitz(t + 1, p, h + 2)
                if not isinstance(h, int) or -1 <= h < NH - 3:
                    if can_wait(h + 2):
                        eng.wait_ge(crev_ready, h + 2)
                    eng.dma_start(c_in[:, 1 - p, :], cg[h + 3]).then_inc(s_c[1 - p], 16)
                if tail:
                    eng.wait_ge(out_ready, h)
                    eng.dma_start(og[h - 1], out_sb[:, 1 - p, :]).then_inc(s_stored[1 - p], 16)

            run(eng, step)
            for p in range(2):
                eng.wait_ge(s_stored[p], 16 * (NH // 2))

        @block.tensor
        def _(eng):
            def transpose4(dst, src, last):
                for c in range(CH):
                    ins = nc.tensor.transpose(dst[:, c * P:(c + 1) * P], src(c), ident)
                ins.then_inc(last, 1)

            def conv(p, lc, h1):
                for mc in range(lc + 1):
                    if lc == mc:
                        eng.wait_ge(kv_ready[mc], h1 + 1)
                    block_t = toep[:, 1 - p, (lc - mc) * P:(lc - mc + 1) * P]
                    nc.tensor.matmul(bank[lc % 2][:, :], block_t, kv[:, 1 - p, mc, 0:FULL],
                                     start=(mc == 0), stop=(mc == lc))
                    ins = nc.tensor.matmul(bank[2][:, lc * HALF:(lc + 1) * HALF], block_t,
                                           kv[:, 1 - p, mc, FULL:FULL + HALF], start=(mc == 0), stop=(mc == lc))
                ins.then_inc(conv_ps[lc], 1)

            eng.wait_ge(s_consts, 16)

            def step(t, p, tail, back, front, pre):
                h = 2 * t + p
                if tail:
                    eng.wait_ge(gated_ready, h)
                    eng.wait_ge(mask_done[2], h)
                    transpose4(bank[6], lambda c: gated[:, c * P:(c + 1) * P], gatedT_ps)
                if front:
                    eng.wait_ge(s_toep[1 - p], 16 * (t + p + 1))
                    if can_wait(h):
                        eng.wait_ge(mask_done[3], h)
                    if can_wait(h + 1):
                        eng.wait_ge(x2_ready, h + 1)
                    conv(p, 0, h + 1)
                    if can_wait(h + 1):
                        eng.wait_ge(mul_done[3], h + 1)
                    conv(p, 1, h + 1)
                if back:
                    eng.wait_ge(z_ready, h + 1)
                    if can_wait(h):
                        eng.wait_ge(mask_done[1], h)
                    transpose4(bank[7], lambda c: z[:, c * P:(c + 1) * P], zT_ps)
                if tail:
                    if pre or front and isinstance(h, int):
                        eng.wait_ge(qx_ready, h + 2)
                    if isinstance(h, int):
                        eng.wait_ge(gate_ready, h)
                        if h == 1:
                            eng.wait_ge(wout_ready, 1)
                    eng.wait_ge(gatedT_sb, h)
                    for c in range(CH):
                        ins = nc.tensor.matmul(bank[5][:, :], gatedT[:, c, :], w_out[:, c, :],
                                               start=(c == 0), stop=(c == CH - 1))
                    ins.then_inc(out_ps, 1)
                if back:
                    if isinstance(h, int) and h == 0:
                        eng.wait_ge(w_ready, 1)
                        eng.wait_ge(s_weights, 64)
                        eng.wait_ge(kx_ready, 2)
                        eng.wait_ge(qx_ready, 2)
                    eng.wait_ge(y_ready, h + 1)
                    if can_wait(h):
                        eng.wait_ge(gatedT_sb, h)
                    for c in range(CH):
                        ins = nc.tensor.matmul(bank[6][:, 0:RH], yT[:, c, :], w_logit[:, c, :],
                                               start=(c == 0), stop=(c == CH - 1))
                    ins.then_inc(logit_ps, 1)
                    for dst, c0, done, free in ((bank[3], 0, qk_ps, mask_done[0]),
                                                (bank[4], 2 * DK, v_ps, o_normed),
                                                (bank[5], 2 * DK + DV, g_ps, out_ready)):
                        if can_wait(h):
                            eng.wait_ge(free, h)
                        for c in range(CH):
                            ins = nc.tensor.matmul(dst[:, :], yT[:, c, :], w_all[:, c, c0:c0 + 512],
                                                   start=(c == 0), stop=(c == CH - 1))
                        ins.then_inc(done, 1)
                if front:
                    eng.wait_ge(mul_done[0], h + 2)
                    conv(p, 2, h + 1)
                if back:
                    eng.wait_ge(u_ready, h + 1)
                    nc.tensor.matmul(bank[6][:, 0:RH], causal, u[:, :], start=True, stop=True).then_inc(cnt_ps, 1)
                if front:
                    eng.wait_ge(mul_done[1], h + 2)
                    conv(p, 3, h + 1)
                if back:
                    eng.wait_ge(ke_ready, h + 1)
                    eng.wait_ge(y_conv, h + 1)
                    transpose4(bank[7], lambda c: ke[:, 4 * c:4 * c + 4, :], keT_ps)
                    eng.wait_ge(qe_ready, h + 1)
                    eng.wait_ge(qk_copied, h + 1)
                    transpose4(bank[3], lambda c: qe[:, 4 * c:4 * c + 4, :], qeT_ps)
                if pre:
                    eng.wait_ge(crev_ready, h + 3)
                    if back:
                        eng.wait_ge(v_copied, h + 1)
                    elif can_wait(h + 2):
                        eng.wait_ge(kx_ready, h + 2)
                    transpose4(bank[4], lambda c: c_rev[:, c, :], cT_ps)
                    eng.wait_ge(qn_ready, h + 3)
                    if back:
                        eng.wait_ge(gate_ready, h + 1)
                    elif can_wait(h + 2):
                        eng.wait_ge(qx_ready, h + 2)
                    transpose4(bank[5], lambda c: qn[:, c * P:(c + 1) * P], qT_ps)
                if back:
                    eng.wait_ge(keT_sb, h + 1)
                    eng.wait_ge(qeT_sb, h + 1)
                    eng.wait_ge(qsel_ready, h + 1)
                    if front:
                        eng.wait_ge(mul_done[2], h + 2)
                    elif can_wait(h):
                        eng.wait_ge(mask_done[3], h)
                    for c in range(CH):
                        for r, b in enumerate((3, 7, 6, 0)):
                            rows = slice(r * 32, r * 32 + 32)
                            ins = nc.tensor.matmul(bank[b][:, c * P:(c + 1) * P], keT[rows, c, :], qeT[rows, c, :],
                                                   start=True, stop=True)
                    ins.then_inc(attn_ps, 1)
                if front:
                    eng.wait_ge(mul_last, h + 2)
                    eng.wait_ge(mul_done[3], h + 2)
                    for c in range(CH):
                        for r in range(8):
                            ins = nc.tensor.matmul(bank[2][:, c * P:(c + 1) * P],
                                                   z_terms[:, c, r * ROW:(r + 1) * ROW], ident,
                                                   is_transpose=True, start=(r == 0), stop=(r == 7))
                    ins.then_inc(xo_ps, 1)
                if back:
                    if pre:
                        eng.wait_ge(kx_ready, h + 3)
                    eng.wait_ge(v_copied, h + 1)
                    for r in range(CH):
                        eng.wait_ge(mask_done[r], h + 1)
                        for c in range(CH):
                            i = 4 * c + r
                            ins = nc.tensor.matmul(bank[4][:, i * HDV:(i + 1) * HDV], att[:, r, c, :],
                                                   v_sb[:, i * HDV:(i + 1) * HDV], start=True, stop=True)
                    ins.then_inc(o_ps, 1)

            run(eng, step)

        @block.scalar
        def _(eng):
            eng.dma_start(gates[:, 0:1], g_xattn.rearrange("(a n) -> a n", a=1).partition_broadcast(P)
                          ).then_inc(s_wout, 16)
            eng.dma_start(gates[:, 1:2], g_ffn.rearrange("(a n) -> a n", a=1).partition_broadcast(P)
                          ).then_inc(s_wout, 16)
            eng.dma_start(w_conv[:, :, :], conv_w.rearrange("(c p) k -> p c k", p=P)).then_inc(s_wout, 16)
            eng.dma_start(router[:, :, :], router_w.rearrange("h v r -> (h v) r").partition_broadcast(P)
                          ).then_inc(s_wout, 16)
            eng.wait_ge(s_wout, 80)
            eng.activation(gates[:, :], gates[:, :], ACT.Tanh).then_inc(gates_ready, 1)
            eng.wait_ge(gates_ready, 1)
            eng.activation(w_out[:, :, :], w_out[:, :, :], ACT.Copy, scale=gates[:, 1:2]).then_inc(wout_ready, 1)

            def step(t, p, tail, back, front, pre):
                h = 2 * t + p
                if pre:
                    eng.wait_ge(s_c[p], 16 * (t + 2))
                    if can_wait(h + 2):
                        eng.wait_ge(cT_ps, h + 2)
                    eng.activation(c_rev[:, :, :], view(c_in[:, p, P - 1:P], [[P, CH], [-1, P]]), ACT.Copy).then_inc(crev_ready, 1)
                if tail:
                    eng.wait_ge(gatedT_ps, h)
                    if can_wait(h - 1):
                        eng.wait_ge(out_ps, h - 1)
                    eng.activation(gatedT[:, :, :], bank[6][:, :].rearrange("p (c n) -> p c n", c=CH), ACT.Copy
                                   ).then_inc(gatedT_sb, 1)
                if back:
                    eng.wait_ge(zT_ps, h + 1)
                    for c in range(CH):
                        ins = eng.activation(y_raw[:, c, :], bank[7][:, c * P:(c + 1) * P], ACT.Copy,
                                             scale=w_conv[:, c, 1:2])
                    ins.then_inc(y_cur, 1)
                    eng.wait_ge(y_conv, h + 1)
                    if can_wait(h):
                        eng.wait_ge(g_ps, h)
                    eng.activation(yT[:, :, :], y_raw[:, :, :], ACT.Silu).then_inc(y_ready, 1)
                    eng.wait_ge(d_ready, h + 1)
                    if can_wait(h):
                        eng.wait_ge(route_a, h)
                    eng.activation(th[:, :], d_log[:, :], ACT.Tanh, scale=0.5).then_inc(th_ready, 1)
                    eng.wait_ge(qk_ps, h + 1)
                    if can_wait(h):
                        eng.wait_ge(rot_prod, 3 * h)
                    eng.activation(qk_sb[:, RH:2 * RH, :], bank[3][:, DK:2 * DK].rearrange("p (a n) -> p a n", n=HDK),
                                   ACT.Copy)
                    eng.activation(qk_sb[:, 0:RH, :], bank[3][:, 0:DK].rearrange("p (a n) -> p a n", n=HDK),
                                   ACT.Silu).then_inc(qk_copied, 1)
                    eng.wait_ge(v_ps, h + 1)
                    if can_wait(h):
                        eng.wait_ge(o_ps, h)
                    eng.activation(v_sb[:, :], bank[4][:, :], ACT.Copy).then_inc(v_copied, 1)
                    eng.wait_ge(g_ps, h + 1)
                    if can_wait(h):
                        eng.wait_ge(gated_ready, h)
                    eng.activation(gate_sb[:, :], bank[5][:, :], ACT.Silu).then_inc(gate_ready, 1)
                    eng.wait_ge(keT_ps, h + 1)
                    if can_wait(h):
                        eng.wait_ge(attn_ps, h)
                    eng.activation(keT[:, :, :], bank[7][:, :].rearrange("p (c n) -> p c n", c=CH), ACT.Copy
                                   ).then_inc(keT_sb, 1)
                    eng.wait_ge(qeT_ps, h + 1)
                    eng.activation(qeT[:, :, :], bank[3][:, :].rearrange("p (c n) -> p c n", c=CH), ACT.Copy
                                   ).then_inc(qeT_sb, 1)
                if pre:
                    for src, dst, ready, done in ((bank[4], kx[:, :, :], cT_ps, kx_ready),
                                                  (bank[5], qx[:, p, :, :], qT_ps, qx_ready)):
                        eng.wait_ge(ready, h + 3)
                        if done is kx_ready and can_wait(h + 2):
                            for c in range(CH):
                                eng.wait_ge(kv_ready[c], h + 2)
                        if done is qx_ready and can_wait(h + 1):
                            eng.wait_ge(mul_last, h + 1)
                            eng.wait_ge(mul_done[CH - 1], h + 1)
                        psum = src[:, :].rearrange("p (c n) -> p c n", c=CH)
                        eng.activation(dst[:, :, 0:ROW], psum, ACT.Copy)
                        eng.activation(dst[:, :, ROW:EXT], psum[:, :, 0:EXT - ROW], ACT.Copy).then_inc(done, 1)
                if back:
                    eng.wait_ge(o_ps, h + 1)
                    if can_wait(h):
                        eng.wait_ge(o_summed, h)
                    eng.activation(o_sq[:, :, :], bank[4][:, :].rearrange("p (a n) -> p a n", n=HDV), ACT.Square
                                   ).then_inc(o_squared, 1)

            run(eng, step)

        @block.gpsimd
        def _(eng):
            eng.memset(minus_half[:, :], -0.5).then_inc(half_ready, 1)
            eng.wait_ge(half_ready, 1)
            eng.wait_ge(s_consts, 16)

            def products(p, c, h2):
                if c == 0:
                    eng.wait_ge(kx_ready, h2 + 1)
                    if can_wait(h2 - 1):
                        eng.wait_ge(conv_ps[CH - 1], h2 - 1)
                eng.tensor_tensor(view(kv[:, p, c, 0:FULL], [[ROW, NROT], [1, ROW]]),
                                  view(kx[:, c, 0:ROW], [[0, NROT], [1, ROW]]),
                                  view(kx[:, c, 0:ROW], [[NB, NROT], [1, ROW]]), ALU.mult)
                eng.tensor_tensor(kv[:, p, c, FULL:FULL + HALF], kx[:, c, 0:HALF],
                                  kx[:, c, HALF:2 * HALF], ALU.mult).then_inc(kv_ready[c], 1)

            def rsqrt(dst, src, n, ready, value, done):
                eng.wait_ge(ready, value)
                eng.tensor_tensor(dst[:, 0:n], src[:, 0:n], minus_half[:, 0:n], ALU.pow).then_inc(done, 1)

            def step(t, p, tail, back, front, pre):
                h = 2 * t + p
                if pre:
                    rsqrt(rstd1, ve1, 1, ve1_ready, h + 3, rstd1_ready)
                if back:
                    eng.wait_ge(qk_copied, h + 1)
                    eng.tensor_tensor(rot_a[:, :, :], qk_sb[:, :, :], view(const[:, C_COS:C_COS + 1], [[0, 2 * RH], [1, HDK]]),
                                      ALU.mult).then_inc(rot_prod, 1)
                    hf = HDK // 2
                    for a in range(2):
                        s = const[:, C_SIN + a * hf:C_SIN + a * hf + 1]
                        eng.tensor_tensor(rot_b[:, :, a * hf:(a + 1) * hf], qk_sb[:, :, (1 - a) * hf:(2 - a) * hf],
                                          view(s, [[0, 2 * RH], [1, hf]]), ALU.mult).then_inc(rot_prod, 1)
                    eng.wait_ge(rot_prod, 3 * h + 3)
                    if can_wait(h):
                        eng.wait_ge(qe_ready, h)
                        eng.wait_ge(ke_ready, h)
                    eng.tensor_tensor(rot[:, :, :], rot_a[:, :, :], rot_b[:, :, :], ALU.add).then_inc(rot_ready, 1)
                if pre:
                    products(p, 0, h + 2)
                if front:
                    rsqrt(rstd2, ve2, 1, ve2_ready, h + 2, rstd2_ready)
                if pre:
                    products(p, 1, h + 2)
                if back:
                    rsqrt(o_rstd, o_ve, RH, o_ve_ready, h + 1, o_rstd_ready)
                if pre:
                    products(p, 2, h + 2)
                    products(p, 3, h + 2)

            run(eng, step)

        @block.vector
        def _(eng):
            eng.memset(taps[0:NH, 0:P], 0.0).then_inc(taps_zero, 1)
            eng.wait_ge(s_taps_in, 32)
            eng.tensor_tensor(taps[0:NH, P:P + 1], taps[0:NH, P:P + 1], d_tap[0:NH, :], ALU.add).then_inc(taps_zero, 1)
            eng.wait_ge(taps_zero, 2)
            eng.memset(u[:, :], 0.0).then_inc(taps_ready, 1)

            def prepare_weights():
                wv = w_all[:, :, 2 * DK:2 * DK + DV]
                eng.wait_ge(s_weights, 64)
                eng.wait_ge(s_wout, 80)
                eng.tensor_tensor(router_d[:, :], router[:, :, 1], router[:, :, 0], ALU.subtract).then_inc(w_step, 1)
                eng.wait_ge(w_step, 1)
                eng.tensor_tensor(w_tmp[:, :, :], wv, view(router_d[:, 0:1], [[0, CH], [1, DV]]), ALU.mult
                                  ).then_inc(w_step, 1)
                eng.wait_ge(w_step, 2)
                eng.tensor_reduce(w_logit[:, :, :].rearrange("p c h -> p (c h)"),
                                  w_tmp[:, :, :].rearrange("p c (h v) -> p (c h) v", v=HDV), AX_X, ALU.add
                                  ).then_inc(w_step, 1)
                for c in range(CH):
                    eng.tensor_reduce(w_mean[:, c, :], wv[:, c, :].rearrange("p (h v) -> p h v", v=HDV), AX_X, ALU.add
                                      ).then_inc(w_step, 1)
                eng.wait_ge(w_step, 3 + CH)
                eng.tensor_scalar(w_mean[:, :, :], w_mean[:, :, :], 1.0 / HDV, None, ALU.mult).then_inc(w_step, 1)
                eng.wait_ge(w_step, 4 + CH)
                for c in range(CH):
                    per_head = wv[:, c, :].rearrange("p (h v) -> p h v", v=HDV)
                    ins = eng.tensor_tensor(per_head, per_head, view(w_mean[:, c, 0:1], [[1, RH], [0, HDV]]), ALU.subtract)
                ins.then_inc(w_ready, 1)

            def multiply(p, lc, h1):
                eng.wait_ge(conv_ps[lc], h1 + 1)
                if lc == 0:
                    eng.wait_ge(qx_ready, h1 + 1)
                    if can_wait(h1):
                        eng.wait_ge(xo_ps, h1)
                q = qx[:, 1 - p, lc, 0:1]
                y = bank[lc % 2]
                eng.tensor_tensor(view(z_terms[:, lc, 0:1], [[ROW, NROT], [1, ROW]]),
                                  view(y[:, 0:1], [[ROW, NROT], [1, ROW]]),
                                  view(q, [[NB, NROT], [1, ROW]]), ALU.mult)
                first = 4 * ROW + NB
                eng.tensor_tensor(view(z_terms[:, lc, first:first + 1], [[ROW + NB, NROT - 1], [1, ROW]]),
                                  view(y[:, ROW:ROW + 1], [[ROW, NROT - 1], [1, ROW]]),
                                  view(q, [[0, NROT - 1], [1, ROW]]), ALU.mult).then_inc(mul_done[lc], 1)

            def multiply_last(p, h1):
                y = view(bank[2][:, 0:1], [[HALF, CH], [NB, 4], [1, NB]])
                q = qx[:, 1 - p, 0, :]
                a, b = 4 * ROW, 7 * ROW + HALF
                eng.tensor_tensor(view(z_terms[:, 0, a:a + 1], [[8 * ROW, CH], [ROW + NB, 4], [1, NB]]), y,
                                  view(q[:, HALF:HALF + 1], [[EXT, CH], [NB, 4], [1, NB]]), ALU.mult)
                eng.tensor_tensor(view(z_terms[:, 0, b:b + 1], [[8 * ROW, CH], [NB, 4], [1, NB]]), y,
                                  view(q[:, 0:1], [[EXT, CH], [NB, 4], [1, NB]]), ALU.mult).then_inc(mul_last, 1)

            def step(t, p, tail, back, front, pre):
                h = 2 * t + p
                if isinstance(h, int) and h == -1:
                    prepare_weights()
                if front:
                    multiply(p, 0, h + 1)
                if back:
                    eng.wait_ge(y_cur, h + 1)
                    for c in range(CH):
                        cur = y_raw[:, c, :].rearrange("p (j l) -> p j l", l=NB)[:, :, 1:NB]
                        prev = bank[7][:, c * P:(c + 1) * P].rearrange("p (j l) -> p j l", l=NB)[:, :, 0:NB - 1]
                        ins = eng.scalar_tensor_tensor(out=cur, in0=prev, scalar=w_conv[:, c, 0:1], in1=cur,
                                                       op0=ALU.mult, op1=ALU.add)
                    ins.then_inc(y_conv, 1)
                if front:
                    multiply(p, 1, h + 1)
                if tail:
                    eng.wait_ge(out_ps, h)
                    if not isinstance(h, int) or h >= 3:
                        eng.wait_ge(s_stored[1 - p], 16 * (t + p - 1))
                    eng.tensor_tensor(out_sb[:, 1 - p, :], bank[5][:, :], x2[:, 1 - p, :], ALU.add
                                      ).then_inc(out_ready, 1)
                if pre:
                    eng.wait_ge(s_x[p], 16 * (t + 2))
                    eng.bn_stats(stats1[:, :], x_in[:, p, :]).then_inc(bn1_done, 1)
                    eng.wait_ge(bn1_done, h + 3)
                    eng.memset(held[:, :], 0.0)
                    eng.bn_aggr(mv1[:, :], stats1[:, :]).then_inc(mv1_done, 1)
                    eng.wait_ge(mv1_done, h + 3)
                    eng.tensor_scalar(ve1[:, :], mv1[:, 1:2], EPS, None, ALU.add).then_inc(ve1_ready, 1)
                if back:
                    eng.wait_ge(logit_ps, h + 1)
                    if can_wait(h):
                        eng.wait_ge(th_ready, h)
                        eng.wait_ge(cnt_ps, h)
                    eng.tensor_copy(d_log[:, :], bank[6][:, 0:RH]).then_inc(d_ready, 1)
                    eng.wait_ge(d_ready, h + 1)
                    eng.tensor_scalar(u[:, :], d_log[:, :], 0.0, 0.5, ALU.is_gt, ALU.subtract).then_inc(u_ready, 1)
                    eng.tensor_scalar(k_sel[:, :, 0], d_log[:, :], 0.0, None, ALU.is_le)
                    eng.tensor_scalar(k_sel[:, :, 1], d_log[:, :], 0.0, None, ALU.is_gt).then_inc(ksel_ready, 1)
                if pre:
                    eng.wait_ge(rstd1_ready, h + 3)
                    if can_wait(h + 2):
                        eng.wait_ge(qT_ps, h + 2)
                    eng.tensor_scalar(qn[:, :], x_in[:, p, :], mv1[:, 0:1], rstd1[:, 0:1], ALU.subtract, ALU.mult
                                      ).then_inc(qn_ready, 1)
                if back:
                    eng.wait_ge(th_ready, h + 1)
                    eng.wait_ge(u_ready, h + 1)
                    eng.tensor_tensor(score[:, :], th[:, :], u[:, :], ALU.mult).then_inc(route_a, 1)
                if front:
                    multiply(p, 2, h + 1)
                if back:
                    eng.wait_ge(cnt_ps, h + 1)
                    eng.tensor_tensor(cnt_a[:, :], u[:, :], bank[6][:, 0:RH], ALU.mult).then_inc(route_b, 1)
                    eng.wait_ge(route_b, 4 * h + 1)
                    eng.tensor_scalar(cnt[:, :], cnt_a[:, :], 2.0, const[:, C_HALF:C_HALF + 1], ALU.mult, ALU.add
                                      ).then_inc(route_b, 1)
                    eng.wait_ge(route_a, h + 1)
                    eng.tensor_scalar(score1[:, :], score[:, :], 0.5, None, ALU.add).then_inc(route_c, 1)
                    eng.wait_ge(route_b, 4 * h + 2)
                    eng.reciprocal(rcnt[:, :], cnt[:, :]).then_inc(route_b, 1)
                    eng.wait_ge(route_b, 4 * h + 3)
                    eng.wait_ge(route_c, h + 1)
                    eng.tensor_tensor(weight[:, :], score1[:, :], rcnt[:, :], ALU.mult).then_inc(route_b, 1)
                    eng.wait_ge(route_b, 4 * h + 4)
                    eng.wait_ge(ksel_ready, h + 1)
                    eng.tensor_tensor(q_sel[:, :, :], view(weight[:, 0:1], [[1, RH], [0, RATIO]]), k_sel[:, :, :],
                                      ALU.mult).then_inc(qsel_ready, 1)
                    eng.wait_ge(rot_ready, h + 1)
                    if can_wait(h):
                        eng.wait_ge(keT_ps, h)
                        eng.wait_ge(qeT_ps, h)
                    for dst, at, sel, done in ((ke, RH, k_sel, ke_ready), (qe, 0, q_sel, qe_ready)):
                        if done is qe_ready:
                            eng.wait_ge(qsel_ready, h + 1)
                        eng.tensor_tensor(view(dst[:, 0, 0:1], [[RATIO * HDK, RH], [HDK, RATIO], [1, HDK]]),
                                          view(rot[:, at, 0:1], [[HDK, RH], [0, RATIO], [1, HDK]]),
                                          view(sel[:, 0, 0:1], [[RATIO, RH], [1, RATIO], [0, HDK]]),
                                          ALU.mult).then_inc(done, 1)
                if front:
                    multiply(p, 3, h + 1)
                    multiply_last(p, h + 1)
                if back:
                    eng.wait_ge(attn_ps, h + 1)
                    if can_wait(h):
                        eng.wait_ge(o_ps, h)
                    for r, b in enumerate((3, 7, 6, 0)):
                        eng.tensor_tensor(att[:, r, :, :], bank[b][:, :].rearrange("p (c n) -> p c n", c=CH),
                                          view(mask[:, 0:1], [[0, CH], [1, P]]), ALU.mult).then_inc(mask_done[r], 1)
                if front:
                    eng.wait_ge(xo_ps, h + 2)
                    if isinstance(h, int) and h == -1:
                        eng.wait_ge(gates_ready, 1)
                    eng.scalar_tensor_tensor(out=x2[:, 1 - p, :], in0=bank[2][:, :], scalar=gates[:, 0:1],
                                             in1=x_in[:, 1 - p, :], op0=ALU.mult, op1=ALU.add).then_inc(x2_ready, 1)
                    eng.wait_ge(x2_ready, h + 2)
                    eng.bn_stats(stats2[:, :], x2[:, 1 - p, :]).then_inc(bn2_done, 1)
                    eng.wait_ge(bn2_done, h + 2)
                    eng.memset(held[:, :], 0.0)
                    eng.bn_aggr(mv2[:, :], stats2[:, :]).then_inc(mv2_done, 1)
                    eng.wait_ge(mv2_done, h + 2)
                    eng.tensor_scalar(ve2[:, :], mv2[:, 1:2], EPS, None, ALU.add).then_inc(ve2_ready, 1)
                if back:
                    eng.wait_ge(o_squared, h + 1)
                    eng.tensor_reduce(o_var[:, :], o_sq[:, :, :], AX_X, ALU.add).then_inc(o_summed, 1)
                    eng.wait_ge(o_summed, h + 1)
                    eng.tensor_scalar(o_ve[:, :], o_var[:, :], 1.0 / HDV, EPS, ALU.mult, ALU.add).then_inc(o_ve_ready, 1)
                if front:
                    eng.wait_ge(rstd2_ready, h + 2)
                    if can_wait(h + 1):
                        eng.wait_ge(zT_ps, h + 1)
                    eng.tensor_scalar(z[:, :], x2[:, 1 - p, :], mv2[:, 0:1], rstd2[:, 0:1], ALU.subtract, ALU.mult
                                      ).then_inc(z_ready, 1)
                if back:
                    eng.wait_ge(o_rstd_ready, h + 1)
                    eng.tensor_tensor(o_n[:, :].rearrange("p (a n) -> p a n", n=HDV),
                                      bank[4][:, :].rearrange("p (a n) -> p a n", n=HDV),
                                      view(o_rstd[:, 0:1], [[1, RH], [0, HDV]]), ALU.mult).then_inc(o_normed, 1)
                    eng.wait_ge(o_normed, h + 1)
                    eng.wait_ge(gate_ready, h + 1)
                    if can_wait(h):
                        eng.wait_ge(gatedT_ps, h)
                    eng.tensor_tensor(gated[:, :], o_n[:, :], gate_sb[:, :], ALU.mult).then_inc(gated_ready, 1)

            run(eng, step)


def shape_constants(NB, HDK):
    p = np.arange(P)
    pos = p % NB
    same = (p[:, None] // NB == p[None, :] // NB) & (pos[:, None] <= pos[None, :])
    inv = (np.float32(1.0) / np.float32(10000.0) ** (np.arange(0, HDK, 2, dtype=np.float32) / np.float32(HDK)))
    f = pos[:, None].astype(np.float32) * inv[None, :].astype(np.float32)
    cos, sin = np.cos(f), np.sin(f)
    parts = [np.eye(P), same * HDK ** -0.5, same, cos, cos, -sin, sin, (pos[:, None] + 1) / 2]
    return np.concatenate([a.astype(np.float32) for a in parts], axis=1)


_NAMES = ["x", "ctx_2048", "g_xattn", "g_ffn", "L0_xattn_ssm_kernel", "L0_xattn_D", "L0_ffn_conv_w", "L0_ffn_Wq",
          "L0_ffn_Wk", "L0_ffn_Wv", "L0_ffn_Wg", "L0_ffn_router_w", "L0_ffn_Wout"]


def kernel(**inputs):
    import concourse.bacc as _bacc
    from concourse.bass_utils import run_bass_kernel_spmd as _run

    nc = _bacc.Bacc("TRN2", target_bir_lowering=False, num_devices=1)
    arrays, args = {}, []
    for name in _NAMES:
        a = np.ascontiguousarray(inputs[name])
        arrays[f"in_{name}"] = a
        args.append(nc.dram_tensor(f"in_{name}", a.shape, mybir.dt.from_np(a.dtype), kind="ExternalInput").ap())
    c = shape_constants(inputs["x"].shape[0], inputs["L0_ffn_Wq"].shape[1] // inputs["L0_ffn_router_w"].shape[0])
    arrays["shape_consts"] = c
    args.append(nc.dram_tensor("shape_consts", c.shape, F32, kind="ExternalInput").ap())
    args.append(nc.dram_tensor("out_x", inputs["x"].shape, F32, kind="ExternalOutput").ap())
    flamingo_gated_layer(nc, *args)
    r = _run(nc, [arrays], core_ids=[0])
    return r.results[0]["out_x"]
```

```python
from contextlib import ExitStack

import numpy as np

import concourse.bass as bass
from concourse import mybir

ALU = mybir.AluOpType
ACT = mybir.ActivationFunctionType
F32 = mybir.dt.float32
F32R = mybir.dt.float32r
AX_X = mybir.AxisListType.X

P = 128
EPS = 1e-5
C_ID, C_MASK, C_CAUSAL, C_COS, C_SIN, C_HALF, C_COLS = 0, 128, 256, 384, 400, 416, 417


def view(ap, dims):
    return bass.AP(tensor=ap.tensor, offset=ap.offset, ap=[ap.ap[0]] + dims)


def can_wait(value):
    return not isinstance(value, int) or value > 0


def flamingo_gated_layer(nc, x, ctx_in, g_xattn, g_ffn, ssm_kernel, ssm_D, conv_w, Wq, Wk, Wv, Wg,
                         router_w, Wout, consts, out):
    NB, ROWS, L = x.shape
    HD = NB // 2
    NH = ROWS // HD
    CH = L // P
    RH, HDV, RATIO = router_w.shape
    DK = Wq.shape[1]
    HDK = DK // RH
    DV = Wv.shape[1]
    NROT = HD // 2
    FULL = NROT * HD * NB
    HALF = HD // 2 * NB
    EXT = (HD + NROT) * NB
    ROW = HD * NB
    K0, LOG0 = DK, 2 * DK
    V0 = LOG0 + RH
    G0 = V0 + DV
    PROJ = G0 + DV

    xg = x.rearrange("b (h j) l -> h j b l", j=HD)
    cg = ctx_in.rearrange("b (h j) l -> h j b l", j=HD)
    og = out.rearrange("b (h j) l -> h j b l", j=HD)
    taps_dram = nc.dram_tensor("taps_dram", (NH, P + L), F32, kind="Internal")

    with ExitStack() as stack:
        def sb(name, *free):
            return stack.enter_context(nc.sbuf_tensor(name, [P, *free], F32))

        def parts(name, *free):
            return [stack.enter_context(nc.sbuf_tensor(f"{name}_{k}", [P, *free], F32R)) for k in ("high", "low")]

        def setup_sb(name, *free):
            return setup.enter_context(nc.sbuf_tensor(name, [P, *free], F32))

        def sem(name):
            return stack.enter_context(nc.semaphore(name))

        const = sb("const", C_COLS)
        w_all_p = parts("w_all", CH, PROJ)
        w_out_p = parts("w_out", CH, L)
        w_conv = sb("w_conv", CH, 2)
        gates = sb("gates", 2)
        d_tap = sb("d_tap", 1)
        w_mean = sb("w_mean", CH, RH)
        minus_half = sb("minus_half", RH)
        x_in = sb("x_in", 2, L)
        c_in = sb("c_in", 2, L)
        c_rev = sb("c_rev", CH, P)
        toep = sb("toep", L)
        held = sb("held", 1)
        stats1 = sb("stats1", 6)
        mv1 = sb("mv1", 2)
        ve1 = sb("ve1", 1)
        rstd1 = sb("rstd1", 1)
        qn = sb("qn", L)
        kx = sb("kx", CH, EXT)
        qx = sb("qx", 2, CH, EXT)
        kv = sb("kv", 2, FULL + HALF)
        kv_p = parts("kv", 2, CH, FULL + HALF)
        toep_p = parts("toep", 2, L)
        z_terms = sb("z_terms", CH, 8 * ROW)
        x2 = sb("x2", 2, L)
        stats2 = sb("stats2", 6)
        mv2 = sb("mv2", 2)
        ve2 = sb("ve2", 1)
        rstd2 = sb("rstd2", 1)
        z = sb("z", L)
        d_log = sb("d_log", RH)
        u = sb("u", RH)
        th = sb("th", RH)
        score = sb("score", RH)
        score1 = sb("score1", RH)
        cnt_a = sb("cnt_a", RH)
        cnt = sb("cnt", RH)
        rcnt = sb("rcnt", RH)
        weight = sb("weight", RH)
        k_sel = sb("k_sel", RH, RATIO)
        q_sel = sb("q_sel", RH, RATIO)
        o_var = sb("o_var", RH)
        o_ve = sb("o_ve", RH)
        o_rstd = sb("o_rstd", RH)

        setup = ExitStack()
        w_all = setup_sb("w_all", CH, PROJ)
        w_out = setup_sb("w_out", CH, L)
        w_tmp = z_terms[:, :, 0:DV]
        router = setup_sb("router", RH * HDV, RATIO)
        router_d = setup_sb("router_d", RH * HDV)
        taps = setup_sb("taps", P + L)
        setup.close()
        y_raw = sb("y_raw", CH, P)
        qk_sb = sb("qk_sb", 2 * RH, HDK)
        rot_a = sb("rot_a", 2 * RH, HDK)
        rot_b = sb("rot_b", 2 * RH, HDK)
        v_sb = sb("v_sb", DV)
        gate_sb = sb("gate_sb", DV)
        qe = sb("qe", RH, RATIO * HDK)
        ke = sb("ke", RH, RATIO * HDK)
        qeT = sb("qeT", CH, P)
        keT = sb("keT", CH, P)
        att = sb("att", CH, CH, P)
        o_sq = sb("o_sq", RH, HDV)
        gated = sb("gated", DV)
        out_sb = sb("out_sb", 2, L)
        yT_p = parts("yT", CH, P)
        gatedT_p = parts("gatedT", CH, P)

        bank = [stack.enter_context(nc.psum_tensor(f"bank{i}", [P, 512], F32)) for i in range(8)]

        ident = const[:, C_ID:C_ID + P]
        mask = const[:, C_MASK:C_MASK + P]
        causal = const[:, C_CAUSAL:C_CAUSAL + P]

        s_taps_in, s_taps_out, s_consts, s_weights, s_wout = (
            sem("s_taps_in"), sem("s_taps_out"), sem("s_consts"), sem("s_weights"), sem("s_wout"))
        s_x = [sem(f"s_x{i}") for i in range(2)]
        s_c = [sem(f"s_c{i}") for i in range(2)]
        s_toep = [sem(f"s_toep{i}") for i in range(2)]
        s_stored = [sem(f"s_stored{i}") for i in range(2)]
        taps_zero, taps_ready, gates_ready, wout_ready = (
            sem("taps_zero"), sem("taps_ready"), sem("gates_ready"), sem("wout_ready"))
        w_step, w_centred, w_high, w_ready, half_ready = (
            sem("w_step"), sem("w_centred"), sem("w_high"), sem("w_ready"), sem("half_ready"))
        conv_last_ps = sem("conv_last_ps")
        gatedT_ps, zT_ps, out_ps, logit_ps, q_ps, v_ps, g_ps, cnt_ps = (
            sem(n) for n in ("gatedT_ps", "zT_ps", "out_ps", "logit_ps", "q_ps", "v_ps", "g_ps", "cnt_ps"))
        conv_ps = [sem(f"conv_ps{i}") for i in range(CH)]
        qeT_ps, keT_ps, cT_ps, qT_ps, attn_ps, xo_ps, o_ps = (
            sem(n) for n in ("qeT_ps", "keT_ps", "cT_ps", "qT_ps", "attn_ps", "xo_ps", "o_ps"))
        gatedT_high, y_cur, y_ready, th_ready, qk_copied, v_copied, gate_ready = (
            sem(n) for n in ("gatedT_high", "y_cur", "y_ready", "th_ready", "qk_copied", "v_copied", "gate_ready"))
        qeT_sb, keT_sb, kx_ready, qx_ready, o_squared = (
            sem(n) for n in ("qeT_sb", "keT_sb", "kx_ready", "qx_ready", "o_squared"))
        crev_ready = sem("crev_ready")
        y_high, toep_high = sem("y_high"), sem("toep_high")
        kv_high = [sem(f"kv_high{i}") for i in range(CH)]
        toep_ready = sem("toep_ready")
        kv_made = [sem(f"kv_made{i}") for i in range(CH)]
        sum_done = [sem(f"sum_done{i}") for i in range(CH)]
        rot_prod, rot_ready, rstd1_ready, rstd2_ready, o_rstd_ready = (
            sem(n) for n in ("rot_prod", "rot_ready", "rstd1_ready", "rstd2_ready", "o_rstd_ready"))
        kv_ready = [sem(f"kv_ready{i}") for i in range(CH)]
        mul_done = [sem(f"mul_done{i}") for i in range(CH)]
        mask_done = [sem(f"mask_done{i}") for i in range(CH)]
        y_low, gatedT_ready, sum_last = sem("y_low"), sem("gatedT_ready"), sem("sum_last")
        (mul_last, y_conv, out_ready, d_ready, u_ready, ksel_ready, route_a, route_b, route_c, qsel_ready,
         q1sel_ready, ke_ready, qe_ready, bn1_done, mv1_done, ve1_ready, qn_ready, x2_ready, bn2_done, mv2_done,
         ve2_ready, z_ready, o_summed, o_ve_ready, o_normed, gated_ready) = (
            sem(n) for n in ("mul_last", "y_conv", "out_ready", "d_ready", "u_ready", "ksel_ready", "route_a",
                             "route_b", "route_c", "qsel_ready", "q1sel_ready", "ke_ready", "qe_ready", "bn1_done",
                             "mv1_done", "ve1_ready", "qn_ready", "x2_ready", "bn2_done", "mv2_done", "ve2_ready",
                             "z_ready", "o_summed", "o_ve_ready", "o_normed", "gated_ready"))

        FIRST, LAST = -2, NH
        LOOP = (2, NH // 2 - 2)

        def run(eng, step):
            def peeled(h):
                step(h // 2, h % 2, 0 <= h - 1, 0 <= h < NH, 0 <= h + 1 < NH, h + 2 < NH)
            for h in range(FIRST, 2 * LOOP[0]):
                peeled(h)
            with eng.Fori(*LOOP) as t:
                for p in range(2):
                    step(t, p, True, True, True, True)
            for h in range(2 * LOOP[1], LAST + 1):
                peeled(h)

        SCORE_BANKS = (0, 7, 5, 3)
        PASSES = ((0, 0), (0, 1), (1, 0))

        block = stack.enter_context(nc.Block())

        @block.sync
        def _(eng):
            eng.dma_start(taps[0:NH, P:P + L], ssm_kernel).then_inc(s_taps_in, 16)
            eng.dma_start(d_tap[0:NH, :], ssm_D.rearrange("(h a) -> h a", a=1)).then_inc(s_taps_in, 16)
            eng.dma_start(const[:, :], consts).then_inc(s_consts, 16)
            eng.dma_start(c_in[:, 0, :], cg[0]).then_inc(s_c[0], 16)
            eng.dma_start(x_in[:, 0, :], xg[0]).then_inc(s_x[0], 16)
            eng.wait_ge(taps_ready, 1)
            eng.dma_start(taps_dram.ap(), taps[0:NH, :]).then_inc(s_taps_out, 16)
            eng.dma_start(c_in[:, 1, :], cg[1]).then_inc(s_c[1], 16)
            for w, c0, cols in ((Wv, V0, DV), (Wq, 0, DK), (Wk, K0, DK), (Wg, G0, DV)):
                eng.dma_start(w_all[:, :, c0:c0 + cols], w.rearrange("(c p) n -> p c n", p=P)).then_inc(s_weights, 16)
            eng.dma_start(w_out[:, :, :], Wout.rearrange("(c p) n -> p c n", p=P)).then_inc(s_wout, 16)
            eng.wait_ge(s_taps_out, 16)

            def toeplitz(t, p, h):
                src = taps_dram.ap()[h, :]
                src = bass.AP(tensor=src.tensor, offset=src.offset + 1, ap=[[1, P], [1, L]])
                eng.dma_start(toep[:, :], src).then_inc(s_toep[p], 16)

            def step(t, p, tail, back, front, pre):
                h = 2 * t + p
                if pre:
                    if not (isinstance(h, int) and h < -1):
                        if can_wait(h + 1):
                            eng.wait_ge(x2_ready, h + 1)
                        eng.dma_start(x_in[:, p, :], xg[h + 2]).then_inc(s_x[p], 16)
                    if can_wait(h + 2):
                        eng.wait_ge(toep_ready, h + 2)
                    toeplitz(t + 1, p, h + 2)
                if not isinstance(h, int) or -1 <= h < NH - 3:
                    if can_wait(h + 2):
                        eng.wait_ge(crev_ready, h + 2)
                    eng.dma_start(c_in[:, 1 - p, :], cg[h + 3]).then_inc(s_c[1 - p], 16)
                if tail:
                    eng.wait_ge(out_ready, h)
                    eng.dma_start(og[h - 1], out_sb[:, 1 - p, :]).then_inc(s_stored[1 - p], 16)

            run(eng, step)
            for p in range(2):
                eng.wait_ge(s_stored[p], 16 * (NH // 2))

        @block.tensor
        def _(eng):
            def transpose4(dst, src, last):
                for c in range(CH):
                    ins = nc.tensor.transpose(dst[:, c * P:(c + 1) * P], src(c), ident)
                ins.then_inc(last, 1)

            def conv(p, lc, h1, between=None):
                for mc in range(lc + 1):
                    if lc == mc:
                        eng.wait_ge(kv_ready[mc], h1 + 1)
                    for i, (a, b) in enumerate(PASSES):
                        ins = nc.tensor.matmul(bank[lc % 2][:, :], toep_p[a][:, 1 - p, (lc - mc) * P:(lc - mc + 1) * P],
                                               kv_p[b][:, 1 - p, mc, 0:FULL],
                                               start=(mc == 0 and i == 0), stop=(mc == lc and i == len(PASSES) - 1))
                        if mc == lc and i == len(PASSES) - 1:
                            ins.then_inc(conv_ps[lc], 1)
                        if between is not None:
                            between(2)

            def conv_last(p, h1):
                eng.wait_ge(kv_ready[CH - 1], h1 + 1)
                for diag in range(CH):
                    for i, (a, b) in enumerate(PASSES):
                        ins = nc.tensor.matmul(bank[2][:, diag * HALF:CH * HALF], toep_p[a][:, 1 - p, diag * P:(diag + 1) * P],
                                               kv_p[b][:, 1 - p, 0:CH - diag, FULL:FULL + HALF],
                                               start=(diag == 0 and i == 0), stop=(diag == CH - 1 and i == len(PASSES) - 1),
                                               skip_group_check=True)
                ins.then_inc(conv_last_ps, 1)

            def project(dst, src_p, w_p, c0, cols, done, low_ready, value):
                for i, (a, b) in enumerate(PASSES):
                    if a == 1:
                        eng.wait_ge(low_ready, value)
                    for c in range(CH):
                        ins = nc.tensor.matmul(dst[:, 0:cols], src_p[a][:, c, :], w_p[b][:, c, c0:c0 + cols],
                                               start=(i == 0 and c == 0), stop=(i == len(PASSES) - 1 and c == CH - 1))
                ins.then_inc(done, 1)

            eng.wait_ge(s_consts, 16)

            def step(t, p, tail, back, front, pre):
                h = 2 * t + p
                todo = list(range(RH)) if tail else []

                def attention_output(n):
                    for k in todo[:n]:
                        r, c = k // CH, k % CH
                        if k == 0:
                            eng.wait_ge(v_copied, h)
                        if c == 0:
                            eng.wait_ge(mask_done[r], h)
                        i = CH * c + r
                        ins = nc.tensor.matmul(bank[4][:, i * HDV:(i + 1) * HDV], att[:, r, c, :],
                                               v_sb[:, i * HDV:(i + 1) * HDV], start=True, stop=True)
                        if k == RH - 1:
                            ins.then_inc(o_ps, 1)
                    del todo[:n]

                if front:
                    eng.wait_ge(toep_ready, h + 2)
                    if can_wait(h):
                        eng.wait_ge(mask_done[0], h)
                    conv(p, 0, h + 1, attention_output)
                    if can_wait(h + 1):
                        eng.wait_ge(mul_done[3], h + 1)
                    conv(p, 1, h + 1, attention_output)
                attention_output(RH)
                if back:
                    eng.wait_ge(z_ready, h + 1)
                    if can_wait(h):
                        eng.wait_ge(mask_done[1], h)
                    transpose4(bank[7], lambda c: z[:, c * P:(c + 1) * P], zT_ps)
                if pre:
                    eng.wait_ge(crev_ready, h + 3)
                    if can_wait(h):
                        eng.wait_ge(mask_done[3], h)
                    elif can_wait(h + 2):
                        eng.wait_ge(kx_ready, h + 2)
                    transpose4(bank[3], lambda c: c_rev[:, c, :], cT_ps)
                if front:
                    eng.wait_ge(mul_done[0], h + 2)
                    conv(p, 2, h + 1)
                    if can_wait(h + 1):
                        eng.wait_ge(x2_ready, h + 1)
                    conv_last(p, h + 1)
                if pre:
                    eng.wait_ge(qn_ready, h + 3)
                    if can_wait(h):
                        eng.wait_ge(qsel_ready, h)
                    elif can_wait(h + 2):
                        eng.wait_ge(qx_ready, h + 2)
                    transpose4(bank[6], lambda c: qn[:, c * P:(c + 1) * P], qT_ps)
                if back:
                    if isinstance(h, int) and h == 0:
                        eng.wait_ge(w_ready, 2)
                    eng.wait_ge(y_high, h + 1)
                    if pre:
                        eng.wait_ge(kx_ready, h + 3)
                    elif can_wait(h):
                        eng.wait_ge(mask_done[3], h)
                    project(bank[3], yT_p, w_all_p, 0, DK, q_ps, y_low, h + 1)
                    if pre:
                        eng.wait_ge(qx_ready, h + 3)
                    elif can_wait(h):
                        eng.wait_ge(qsel_ready, h)
                    project(bank[6], yT_p, w_all_p, K0, DK + RH, logit_ps, y_low, h + 1)
                    if can_wait(h):
                        eng.wait_ge(o_normed, h)
                    project(bank[4], yT_p, w_all_p, V0, DV, v_ps, y_low, h + 1)
                    eng.wait_ge(u_ready, h + 1)
                    eng.wait_ge(qk_copied, h + 1)
                    nc.tensor.matmul(bank[6][:, 0:RH], causal, u[:, :], start=True, stop=True).then_inc(cnt_ps, 1)
                if tail:
                    eng.wait_ge(gated_ready, h)
                    if back:
                        eng.wait_ge(y_conv, h + 1)
                    else:
                        eng.wait_ge(mask_done[1], h)
                    transpose4(bank[7], lambda c: gated[:, c * P:(c + 1) * P], gatedT_ps)
                if back:
                    if can_wait(h):
                        eng.wait_ge(mask_done[2], h)
                    project(bank[5], yT_p, w_all_p, G0, DV, g_ps, y_low, h + 1)
                if tail:
                    eng.wait_ge(gatedT_high, h)
                    if front:
                        eng.wait_ge(mul_done[1], h + 2)
                    else:
                        eng.wait_ge(out_ready, h - 1)
                        if back:
                            eng.wait_ge(mul_done[3], h + 1)
                    project(bank[1], gatedT_p, w_out_p, 0, L, out_ps, gatedT_ready, h)
                if back:
                    eng.wait_ge(ke_ready, h + 1)
                    eng.wait_ge(gate_ready, h + 1)
                    transpose4(bank[5], lambda c: ke[:, 4 * c:4 * c + 4, :], keT_ps)
                    eng.wait_ge(qe_ready, h + 1)
                    transpose4(bank[3], lambda c: qe[:, 4 * c:4 * c + 4, :], qeT_ps)
                if front:
                    if tail:
                        eng.wait_ge(out_ready, h)
                    else:
                        eng.wait_ge(mul_done[1], h + 2)
                    conv(p, 3, h + 1)
                if back:
                    eng.wait_ge(keT_sb, h + 1)
                    eng.wait_ge(qeT_sb, h + 1)
                    if tail:
                        eng.wait_ge(gatedT_ready, h)
                    if front:
                        eng.wait_ge(mul_done[2], h + 2)
                    elif can_wait(h):
                        eng.wait_ge(mask_done[0], h)
                    for c in range(CH):
                        for r, b in enumerate(SCORE_BANKS):
                            rows = slice(r * 32, r * 32 + 32)
                            ins = nc.tensor.matmul(bank[b][:, c * P:(c + 1) * P], keT[rows, c, :], qeT[rows, c, :],
                                                   start=True, stop=True)
                    ins.then_inc(attn_ps, 1)
                if front:
                    for c in range(CH):
                        eng.wait_ge(sum_done[c], h + 2)
                    eng.wait_ge(sum_last, h + 2)
                    for c in range(CH):
                        for i, r in enumerate((0, 1, 4, 5)):
                            ins = nc.tensor.matmul(bank[2][:, c * P:(c + 1) * P],
                                                   z_terms[:, c, r * ROW:(r + 1) * ROW], ident,
                                                   is_transpose=True, start=(i == 0), stop=(i == 3))
                    ins.then_inc(xo_ps, 1)

            run(eng, step)

        @block.scalar
        def _(eng):
            eng.dma_start(gates[:, 0:1], g_xattn.rearrange("(a n) -> a n", a=1).partition_broadcast(P)
                          ).then_inc(s_wout, 16)
            eng.dma_start(gates[:, 1:2], g_ffn.rearrange("(a n) -> a n", a=1).partition_broadcast(P)
                          ).then_inc(s_wout, 16)
            eng.dma_start(w_conv[:, :, :], conv_w.rearrange("(c p) k -> p c k", p=P)).then_inc(s_wout, 16)
            eng.dma_start(router[:, :, :], router_w.rearrange("h v r -> (h v) r").partition_broadcast(P)
                          ).then_inc(s_wout, 16)
            eng.wait_ge(s_wout, 80)
            eng.activation(gates[:, :], gates[:, :], ACT.Tanh).then_inc(gates_ready, 1)
            eng.wait_ge(gates_ready, 1)
            eng.activation(w_out[:, :, :], w_out[:, :, :], ACT.Copy, scale=gates[:, 1:2]).then_inc(wout_ready, 1)
            eng.wait_ge(wout_ready, 1)
            eng.activation(w_out_p[0][:, :, :], w_out[:, :, :], ACT.Copy).then_inc(w_high, 1)

            def split_weights():
                eng.wait_ge(w_centred, 1)
                eng.activation(w_all_p[0][:, :, :], w_all[:, :, :], ACT.Copy).then_inc(w_high, 1)

            def extend(dst, src, done):
                psum = src[:, :].rearrange("p (c n) -> p c n", c=CH)
                eng.activation(dst[:, :, 0:ROW], psum, ACT.Copy)
                eng.activation(dst[:, :, ROW:EXT], psum[:, :, 0:EXT - ROW], ACT.Copy).then_inc(done, 1)

            def kv_round(p, c, h2):
                eng.wait_ge(kv_made[c], h2 + 1)
                if can_wait(h2 - 1):
                    eng.wait_ge(conv_ps[CH - 1], h2 - 1)
                    eng.wait_ge(conv_last_ps, h2 - 1)
                eng.activation(kv_p[0][:, p, c, :], kv[:, c % 2, :], ACT.Copy).then_inc(kv_high[c], 1)

            def step(t, p, tail, back, front, pre):
                h = 2 * t + p
                if isinstance(h, int) and h == -1:
                    split_weights()
                if pre:
                    eng.wait_ge(s_c[p], 16 * (t + 2))
                    if can_wait(h + 2):
                        eng.wait_ge(cT_ps, h + 2)
                    eng.activation(c_rev[:, :, :], view(c_in[:, p, P - 1:P], [[P, CH], [-1, P]]), ACT.Copy
                                   ).then_inc(crev_ready, 1)
                if tail:
                    eng.wait_ge(o_ps, h)
                    if can_wait(h - 1):
                        eng.wait_ge(o_summed, h - 1)
                    eng.activation(o_sq[:, :, :], bank[4][:, :].rearrange("p (a n) -> p a n", n=HDV), ACT.Square
                                   ).then_inc(o_squared, 1)
                if back:
                    eng.wait_ge(zT_ps, h + 1)
                    if can_wait(h):
                        eng.wait_ge(y_low, h)
                    elif isinstance(h, int):
                        eng.wait_ge(w_ready, 2)
                    for c in range(CH):
                        ins = eng.activation(y_raw[:, c, :], bank[7][:, c * P:(c + 1) * P], ACT.Copy,
                                             scale=w_conv[:, c, 1:2])
                    ins.then_inc(y_cur, 1)
                if pre:
                    eng.wait_ge(cT_ps, h + 3)
                    if can_wait(h + 2):
                        for c in range(CH):
                            eng.wait_ge(kv_made[c], h + 2)
                    extend(kx[:, :, :], bank[3], kx_ready)
                if back:
                    eng.wait_ge(y_conv, h + 1)
                    if can_wait(h):
                        eng.wait_ge(g_ps, h)
                    eng.activation(yT_p[0][:, :, :], y_raw[:, :, :], ACT.Silu).then_inc(y_high, 1)
                if back:
                    eng.wait_ge(y_high, h + 1)
                    eng.activation(y_raw[:, :, :], y_raw[:, :, :], ACT.Silu).then_inc(y_ready, 1)
                if pre:
                    eng.wait_ge(qT_ps, h + 3)
                    if can_wait(h + 1):
                        eng.wait_ge(mul_last, h + 1)
                        eng.wait_ge(mul_done[CH - 1], h + 1)
                    extend(qx[:, p, :, :], bank[6], qx_ready)
                if pre:
                    kv_round(p, 0, h + 2)
                if back:
                    eng.wait_ge(q_ps, h + 1)
                    if can_wait(h):
                        eng.wait_ge(rot_prod, 3 * h)
                    eng.activation(qk_sb[:, 0:RH, :], bank[3][:, 0:DK].rearrange("p (a n) -> p a n", n=HDK),
                                   ACT.Silu)
                    eng.wait_ge(logit_ps, h + 1)
                    eng.activation(qk_sb[:, RH:2 * RH, :], bank[6][:, 0:DK].rearrange("p (a n) -> p a n", n=HDK),
                                   ACT.Copy).then_inc(qk_copied, 1)
                    eng.wait_ge(d_ready, h + 1)
                    if can_wait(h):
                        eng.wait_ge(route_a, h)
                    eng.activation(th[:, :], d_log[:, :], ACT.Tanh, scale=0.5).then_inc(th_ready, 1)
                if pre:
                    kv_round(p, 1, h + 2)
                if back:
                    eng.wait_ge(v_ps, h + 1)
                    if can_wait(h):
                        eng.wait_ge(o_ps, h)
                    eng.activation(v_sb[:, :], bank[4][:, :], ACT.Copy).then_inc(v_copied, 1)
                if tail:
                    eng.wait_ge(gatedT_ps, h)
                    if can_wait(h - 1):
                        eng.wait_ge(out_ps, h - 1)
                    eng.activation(gatedT_p[0][:, :, :], bank[7][:, :].rearrange("p (c n) -> p c n", c=CH), ACT.Copy
                                   ).then_inc(gatedT_high, 1)
                if back:
                    eng.wait_ge(g_ps, h + 1)
                    if can_wait(h):
                        eng.wait_ge(gated_ready, h)
                    eng.activation(gate_sb[:, :], bank[5][:, :], ACT.Silu).then_inc(gate_ready, 1)
                if pre:
                    kv_round(p, 2, h + 2)
                    eng.wait_ge(s_toep[p], 16 * (t + 2))
                    eng.activation(toep_p[0][:, p, :], toep[:, :], ACT.Copy).then_inc(toep_high, 1)
                if back:
                    eng.wait_ge(keT_ps, h + 1)
                    if can_wait(h):
                        eng.wait_ge(attn_ps, h)
                    eng.activation(keT[:, :, :], bank[5][:, :].rearrange("p (c n) -> p c n", c=CH), ACT.Copy
                                   ).then_inc(keT_sb, 1)
                    eng.wait_ge(qeT_ps, h + 1)
                    eng.activation(qeT[:, :, :], bank[3][:, :].rearrange("p (c n) -> p c n", c=CH), ACT.Copy
                                   ).then_inc(qeT_sb, 1)
                if pre:
                    kv_round(p, 3, h + 2)

            run(eng, step)

        @block.gpsimd
        def _(eng):
            eng.memset(minus_half[:, :], -0.5).then_inc(half_ready, 1)
            eng.wait_ge(half_ready, 1)
            eng.wait_ge(s_consts, 16)

            def products(p, c, h2):
                if c == 0:
                    eng.wait_ge(kx_ready, h2 + 1)
                if c >= 2:
                    eng.wait_ge(kv_ready[c - 2], h2 + 1)
                elif can_wait(h2):
                    eng.wait_ge(kv_ready[c + 2], h2)
                eng.tensor_tensor(view(kv[:, c % 2, 0:FULL], [[ROW, NROT], [1, ROW]]),
                                  view(kx[:, c, 0:ROW], [[0, NROT], [1, ROW]]),
                                  view(kx[:, c, 0:ROW], [[NB, NROT], [1, ROW]]), ALU.mult)
                eng.tensor_tensor(kv[:, c % 2, FULL:FULL + HALF], kx[:, c, 0:HALF],
                                  kx[:, c, HALF:2 * HALF], ALU.mult).then_inc(kv_made[c], 1)

            def kv_rest(p, c, h2):
                eng.wait_ge(kv_high[c], h2 + 1)
                eng.tensor_tensor(kv_p[1][:, p, c, :], kv[:, c % 2, :], kv_p[0][:, p, c, :].bitcast(F32), ALU.subtract
                                  ).then_inc(kv_ready[c], 1)

            def add_terms(lc, h1):
                eng.wait_ge(mul_done[lc], h1 + 1)
                eng.tensor_tensor(z_terms[:, lc, 0:2 * ROW], z_terms[:, lc, 0:2 * ROW], z_terms[:, lc, 2 * ROW:4 * ROW],
                                  ALU.add).then_inc(sum_done[lc], 1)

            def rsqrt(dst, src, n, ready, value, done):
                eng.wait_ge(ready, value)
                eng.tensor_tensor(dst[:, 0:n], src[:, 0:n], minus_half[:, 0:n], ALU.pow).then_inc(done, 1)

            def step(t, p, tail, back, front, pre):
                h = 2 * t + p
                if pre:
                    rsqrt(rstd1, ve1, 1, ve1_ready, h + 3, rstd1_ready)
                if tail:
                    rsqrt(o_rstd, o_ve, RH, o_ve_ready, h, o_rstd_ready)
                if pre:
                    products(p, 0, h + 2)
                if front:
                    add_terms(0, h + 1)
                    add_terms(1, h + 1)
                if pre:
                    products(p, 1, h + 2)
                    kv_rest(p, 0, h + 2)
                if back:
                    eng.wait_ge(qk_copied, h + 1)
                    if can_wait(h):
                        eng.wait_ge(qe_ready, h)
                        eng.wait_ge(ke_ready, h)
                    eng.tensor_tensor(rot_a[:, :, :], qk_sb[:, :, :], view(const[:, C_COS:C_COS + 1], [[0, 2 * RH], [1, HDK]]),
                                      ALU.mult).then_inc(rot_prod, 1)
                    hf = HDK // 2
                    for a in range(2):
                        s = const[:, C_SIN + a * hf:C_SIN + a * hf + 1]
                        eng.tensor_tensor(rot_b[:, :, a * hf:(a + 1) * hf], qk_sb[:, :, (1 - a) * hf:(2 - a) * hf],
                                          view(s, [[0, 2 * RH], [1, hf]]), ALU.mult).then_inc(rot_prod, 1)
                    eng.wait_ge(rot_prod, 3 * h + 3)
                    eng.tensor_tensor(rot_a[:, :, :], rot_a[:, :, :], rot_b[:, :, :], ALU.add).then_inc(rot_ready, 1)
                if front:
                    add_terms(2, h + 1)
                if pre:
                    kv_rest(p, 1, h + 2)
                    products(p, 2, h + 2)
                    products(p, 3, h + 2)
                    kv_rest(p, 2, h + 2)
                    eng.wait_ge(toep_high, h + 3)
                    if can_wait(h + 1):
                        eng.wait_ge(conv_ps[CH - 1], h + 1)
                    eng.tensor_tensor(toep_p[1][:, p, :], toep[:, :], toep_p[0][:, p, :].bitcast(F32), ALU.subtract
                                      ).then_inc(toep_ready, 1)
                if front:
                    add_terms(3, h + 1)
                if pre:
                    kv_rest(p, 3, h + 2)
                if front:
                    rsqrt(rstd2, ve2, 1, ve2_ready, h + 2, rstd2_ready)

            run(eng, step)

        @block.vector
        def _(eng):
            eng.memset(taps[0:NH, 0:P], 0.0).then_inc(taps_zero, 1)
            eng.wait_ge(s_taps_in, 32)
            eng.tensor_tensor(taps[0:NH, P:P + 1], taps[0:NH, P:P + 1], d_tap[0:NH, :], ALU.add).then_inc(taps_zero, 1)
            eng.wait_ge(taps_zero, 2)
            eng.memset(u[:, :], 0.0).then_inc(taps_ready, 1)

            def prepare_weights():
                wv = w_all[:, :, V0:V0 + DV]
                eng.wait_ge(s_weights, 64)
                eng.wait_ge(s_wout, 80)
                eng.tensor_tensor(router_d[:, :], router[:, :, 1], router[:, :, 0], ALU.subtract).then_inc(w_step, 1)
                eng.wait_ge(w_step, 1)
                eng.tensor_tensor(w_tmp, wv, view(router_d[:, 0:1], [[0, CH], [1, DV]]), ALU.mult
                                  ).then_inc(w_step, 1)
                eng.wait_ge(w_step, 2)
                for c in range(CH):
                    eng.tensor_reduce(w_all[:, c, LOG0:LOG0 + RH],
                                  w_tmp[:, c, :].rearrange("p (h v) -> p h v", v=HDV), AX_X, ALU.add
                                      ).then_inc(w_step, 1)
                for c in range(CH):
                    eng.tensor_reduce(w_mean[:, c, :], wv[:, c, :].rearrange("p (h v) -> p h v", v=HDV), AX_X, ALU.add
                                      ).then_inc(w_step, 1)
                eng.wait_ge(w_step, 2 + 2 * CH)
                eng.tensor_scalar(w_mean[:, :, :], w_mean[:, :, :], 1.0 / HDV, None, ALU.mult).then_inc(w_step, 1)
                eng.wait_ge(w_step, 3 + 2 * CH)
                for c in range(CH):
                    per_head = wv[:, c, :].rearrange("p (h v) -> p h v", v=HDV)
                    ins = eng.tensor_tensor(per_head, per_head, view(w_mean[:, c, 0:1], [[1, RH], [0, HDV]]), ALU.subtract)
                ins.then_inc(w_centred, 1)
                for whole, part, n in ((w_out, w_out_p, 1), (w_all, w_all_p, 2)):
                    eng.wait_ge(w_high, n)
                    eng.tensor_tensor(part[1][:, :, :], whole[:, :, :], part[0][:, :, :].bitcast(F32), ALU.subtract
                                      ).then_inc(w_ready, 1)

            def multiply(p, lc, h1):
                eng.wait_ge(conv_ps[lc], h1 + 1)
                if lc == 0:
                    eng.wait_ge(qx_ready, h1 + 1)
                    if can_wait(h1):
                        eng.wait_ge(xo_ps, h1)
                q = qx[:, 1 - p, lc, 0:1]
                y = bank[lc % 2]
                eng.tensor_tensor(view(z_terms[:, lc, 0:1], [[ROW, NROT], [1, ROW]]),
                                  view(y[:, 0:1], [[ROW, NROT], [1, ROW]]),
                                  view(q, [[NB, NROT], [1, ROW]]), ALU.mult)
                first = 4 * ROW + NB
                eng.tensor_tensor(view(z_terms[:, lc, first:first + 1], [[ROW + NB, NROT - 1], [1, ROW]]),
                                  view(y[:, ROW:ROW + 1], [[ROW, NROT - 1], [1, ROW]]),
                                  view(q, [[0, NROT - 1], [1, ROW]]), ALU.mult).then_inc(mul_done[lc], 1)

            def expand(dst, at, sel, done):
                eng.tensor_tensor(view(dst[:, 0, 0:1], [[RATIO * HDK, RH], [HDK, RATIO], [1, HDK]]),
                                  view(rot_a[:, at, 0:1], [[HDK, RH], [0, RATIO], [1, HDK]]),
                                  view(sel[:, 0, 0:1], [[RATIO, RH], [1, RATIO], [0, HDK]]),
                                  ALU.mult).then_inc(done, 1)

            def multiply_last(p, h1):
                eng.wait_ge(conv_last_ps, h1 + 1)
                y = view(bank[2][:, 0:1], [[HALF, CH], [NB, 4], [1, NB]])
                q = qx[:, 1 - p, 0, :]
                a, b = 4 * ROW, 7 * ROW + HALF
                eng.tensor_tensor(view(z_terms[:, 0, a:a + 1], [[8 * ROW, CH], [ROW + NB, 4], [1, NB]]), y,
                                  view(q[:, HALF:HALF + 1], [[EXT, CH], [NB, 4], [1, NB]]), ALU.mult)
                eng.tensor_tensor(view(z_terms[:, 0, b:b + 1], [[8 * ROW, CH], [NB, 4], [1, NB]]), y,
                                  view(q[:, 0:1], [[EXT, CH], [NB, 4], [1, NB]]), ALU.mult).then_inc(mul_last, 1)

            def step(t, p, tail, back, front, pre):
                h = 2 * t + p
                if isinstance(h, int) and h == -1:
                    prepare_weights()
                if front:
                    multiply(p, 0, h + 1)
                if pre:
                    eng.wait_ge(s_x[p], 16 * (t + 2))
                    eng.bn_stats(stats1[:, :], x_in[:, p, :]).then_inc(bn1_done, 1)
                    eng.wait_ge(bn1_done, h + 3)
                    eng.memset(held[:, :], 0.0)
                    eng.bn_aggr(mv1[:, :], stats1[:, :]).then_inc(mv1_done, 1)
                    eng.wait_ge(mv1_done, h + 3)
                    eng.tensor_scalar(ve1[:, :], mv1[:, 1:2], EPS, None, ALU.add).then_inc(ve1_ready, 1)
                if tail:
                    eng.wait_ge(o_squared, h)
                    eng.tensor_reduce(o_var[:, :], o_sq[:, :, :], AX_X, ALU.add).then_inc(o_summed, 1)
                    eng.wait_ge(o_summed, h)
                    eng.tensor_scalar(o_ve[:, :], o_var[:, :], 1.0 / HDV, EPS, ALU.mult, ALU.add).then_inc(o_ve_ready, 1)
                if back:
                    eng.wait_ge(y_cur, h + 1)
                    for c in range(CH):
                        cur = y_raw[:, c, :].rearrange("p (j l) -> p j l", l=NB)[:, :, 1:NB]
                        prev = bank[7][:, c * P:(c + 1) * P].rearrange("p (j l) -> p j l", l=NB)[:, :, 0:NB - 1]
                        ins = eng.scalar_tensor_tensor(out=cur, in0=prev, scalar=w_conv[:, c, 0:1], in1=cur,
                                                       op0=ALU.mult, op1=ALU.add)
                    ins.then_inc(y_conv, 1)
                if pre:
                    eng.wait_ge(rstd1_ready, h + 3)
                    if can_wait(h + 2):
                        eng.wait_ge(qT_ps, h + 2)
                    eng.tensor_scalar(qn[:, :], x_in[:, p, :], mv1[:, 0:1], rstd1[:, 0:1], ALU.subtract, ALU.mult
                                      ).then_inc(qn_ready, 1)
                if front:
                    multiply(p, 1, h + 1)
                if back:
                    eng.wait_ge(y_high, h + 1)
                    eng.wait_ge(y_ready, h + 1)
                    eng.tensor_tensor(yT_p[1][:, :, :], y_raw[:, :, :], yT_p[0][:, :, :].bitcast(F32), ALU.subtract
                                      ).then_inc(y_low, 1)
                if tail:
                    eng.wait_ge(o_rstd_ready, h)
                    if can_wait(h - 1):
                        eng.wait_ge(gatedT_ps, h - 1)
                    eng.tensor_tensor(gated[:, :].rearrange("p (a n) -> p a n", n=HDV),
                                      bank[4][:, :].rearrange("p (a n) -> p a n", n=HDV),
                                      view(o_rstd[:, 0:1], [[1, RH], [0, HDV]]), ALU.mult).then_inc(o_normed, 1)
                    eng.wait_ge(o_normed, h)
                    eng.wait_ge(gate_ready, h)
                    eng.tensor_tensor(gated[:, :], gated[:, :], gate_sb[:, :], ALU.mult).then_inc(gated_ready, 1)
                if front:
                    multiply(p, 2, h + 1)
                    multiply_last(p, h + 1)
                if back:
                    eng.wait_ge(logit_ps, h + 1)
                    if can_wait(h):
                        eng.wait_ge(th_ready, h)
                        eng.wait_ge(cnt_ps, h)
                    eng.wait_ge(qk_copied, h + 1)
                    eng.tensor_copy(d_log[:, :], bank[6][:, DK:DK + RH]).then_inc(d_ready, 1)
                    eng.wait_ge(d_ready, h + 1)
                    eng.tensor_scalar(u[:, :], d_log[:, :], 0.0, 0.5, ALU.is_gt, ALU.subtract).then_inc(u_ready, 1)
                    eng.tensor_scalar(k_sel[:, :, 0], d_log[:, :], 0.0, None, ALU.is_le)
                    eng.tensor_scalar(k_sel[:, :, 1], d_log[:, :], 0.0, None, ALU.is_gt).then_inc(ksel_ready, 1)
                    eng.wait_ge(th_ready, h + 1)
                    eng.wait_ge(u_ready, h + 1)
                    eng.tensor_tensor(score[:, :], th[:, :], u[:, :], ALU.mult).then_inc(route_a, 1)
                    eng.wait_ge(route_a, h + 1)
                    eng.tensor_scalar(score1[:, :], score[:, :], 0.5, None, ALU.add).then_inc(route_c, 1)
                if tail:
                    eng.wait_ge(gatedT_high, h)
                    eng.tensor_tensor(gatedT_p[1][:, :, :], bank[7][:, :].rearrange("p (c n) -> p c n", c=CH),
                                      gatedT_p[0][:, :, :].bitcast(F32), ALU.subtract).then_inc(gatedT_ready, 1)
                if back:
                    eng.wait_ge(rot_ready, h + 1)
                    eng.wait_ge(ksel_ready, h + 1)
                    if can_wait(h):
                        eng.wait_ge(keT_ps, h)
                        eng.wait_ge(qeT_ps, h)
                    expand(ke, RH, k_sel, ke_ready)
                if back:
                    eng.wait_ge(cnt_ps, h + 1)
                    eng.tensor_tensor(cnt_a[:, :], u[:, :], bank[6][:, 0:RH], ALU.mult).then_inc(route_b, 1)
                    eng.wait_ge(route_b, 4 * h + 1)
                    eng.tensor_scalar(cnt[:, :], cnt_a[:, :], 2.0, const[:, C_HALF:C_HALF + 1], ALU.mult, ALU.add
                                      ).then_inc(route_b, 1)
                    eng.wait_ge(route_b, 4 * h + 2)
                    eng.reciprocal(rcnt[:, :], cnt[:, :]).then_inc(route_b, 1)
                    eng.wait_ge(route_b, 4 * h + 3)
                    eng.wait_ge(route_c, h + 1)
                    eng.tensor_tensor(weight[:, :], score1[:, :], rcnt[:, :], ALU.mult).then_inc(route_b, 1)
                    eng.wait_ge(route_b, 4 * h + 4)
                    eng.tensor_tensor(q_sel[:, :, :], view(weight[:, 0:1], [[1, RH], [0, RATIO]]), k_sel[:, :, :],
                                      ALU.mult).then_inc(qsel_ready, 1)
                    eng.wait_ge(qsel_ready, h + 1)
                    expand(qe, 0, q_sel, qe_ready)
                if tail:
                    eng.wait_ge(out_ps, h)
                    if not isinstance(h, int) or h >= 3:
                        eng.wait_ge(s_stored[1 - p], 16 * (t + p - 1))
                    eng.tensor_tensor(out_sb[:, 1 - p, :], bank[1][:, :], x2[:, 1 - p, :], ALU.add
                                      ).then_inc(out_ready, 1)
                if front:
                    multiply(p, 3, h + 1)
                    eng.wait_ge(mul_last, h + 2)
                    eng.wait_ge(mul_done[CH - 1], h + 2)
                    eng.tensor_tensor(z_terms[:, :, 4 * ROW:6 * ROW], z_terms[:, :, 4 * ROW:6 * ROW],
                                      z_terms[:, :, 6 * ROW:8 * ROW], ALU.add).then_inc(sum_last, 1)
                if back:
                    eng.wait_ge(attn_ps, h + 1)
                    if can_wait(h):
                        eng.wait_ge(o_ps, h)
                    for r, b in enumerate(SCORE_BANKS):
                        eng.tensor_tensor(att[:, r, :, :], bank[b][:, :].rearrange("p (c n) -> p c n", c=CH),
                                          view(mask[:, 0:1], [[0, CH], [1, P]]), ALU.mult).then_inc(mask_done[r], 1)
                if front:
                    eng.wait_ge(xo_ps, h + 2)
                    if isinstance(h, int) and h == -1:
                        eng.wait_ge(gates_ready, 1)
                    eng.scalar_tensor_tensor(out=x2[:, 1 - p, :], in0=bank[2][:, :], scalar=gates[:, 0:1],
                                             in1=x_in[:, 1 - p, :], op0=ALU.mult, op1=ALU.add).then_inc(x2_ready, 1)
                    eng.wait_ge(x2_ready, h + 2)
                    eng.bn_stats(stats2[:, :], x2[:, 1 - p, :]).then_inc(bn2_done, 1)
                    eng.wait_ge(bn2_done, h + 2)
                    eng.memset(held[:, :], 0.0)
                    eng.bn_aggr(mv2[:, :], stats2[:, :]).then_inc(mv2_done, 1)
                    eng.wait_ge(mv2_done, h + 2)
                    eng.tensor_scalar(ve2[:, :], mv2[:, 1:2], EPS, None, ALU.add).then_inc(ve2_ready, 1)
                    eng.wait_ge(rstd2_ready, h + 2)
                    if can_wait(h + 1):
                        eng.wait_ge(zT_ps, h + 1)
                    eng.tensor_scalar(z[:, :], x2[:, 1 - p, :], mv2[:, 0:1], rstd2[:, 0:1], ALU.subtract, ALU.mult
                                      ).then_inc(z_ready, 1)

            run(eng, step)


def shape_constants(NB, HDK):
    p = np.arange(P)
    pos = p % NB
    same = (p[:, None] // NB == p[None, :] // NB) & (pos[:, None] <= pos[None, :])
    inv = (np.float32(1.0) / np.float32(10000.0) ** (np.arange(0, HDK, 2, dtype=np.float32) / np.float32(HDK)))
    f = pos[:, None].astype(np.float32) * inv[None, :].astype(np.float32)
    cos, sin = np.cos(f), np.sin(f)
    parts = [np.eye(P), same * HDK ** -0.5, same, cos, cos, -sin, sin, (pos[:, None] + 1) / 2]
    return np.concatenate([a.astype(np.float32) for a in parts], axis=1)


_NAMES = ["x", "ctx_2048", "g_xattn", "g_ffn", "L0_xattn_ssm_kernel", "L0_xattn_D", "L0_ffn_conv_w", "L0_ffn_Wq",
          "L0_ffn_Wk", "L0_ffn_Wv", "L0_ffn_Wg", "L0_ffn_router_w", "L0_ffn_Wout"]


def kernel(**inputs):
    import concourse.bacc as _bacc
    from concourse.bass_utils import run_bass_kernel_spmd as _run

    nc = _bacc.Bacc("TRN2", target_bir_lowering=False, num_devices=1)
    arrays, args = {}, []
    for name in _NAMES:
        a = np.ascontiguousarray(inputs[name])
        arrays[f"in_{name}"] = a
        args.append(nc.dram_tensor(f"in_{name}", a.shape, mybir.dt.from_np(a.dtype), kind="ExternalInput").ap())
    c = shape_constants(inputs["x"].shape[0], inputs["L0_ffn_Wq"].shape[1] // inputs["L0_ffn_router_w"].shape[0])
    arrays["shape_consts"] = c
    args.append(nc.dram_tensor("shape_consts", c.shape, F32, kind="ExternalInput").ap())
    args.append(nc.dram_tensor("out_x", inputs["x"].shape, F32, kind="ExternalOutput").ap())
    flamingo_gated_layer(nc, *args)
    r = _run(nc, [arrays], core_ids=[0])
    return r.results[0]["out_x"]
```

```python
from contextlib import ExitStack

import numpy as np

import concourse.bass as bass
from concourse import mybir

ALU = mybir.AluOpType
ACT = mybir.ActivationFunctionType
F32 = mybir.dt.float32
F32R = mybir.dt.float32r
AX_X = mybir.AxisListType.X

P = 128
EPS = 1e-5
C_ID, C_MASK, C_CAUSAL, C_COS, C_SIN, C_HALF, C_COLS = 0, 128, 256, 384, 400, 416, 417


def view(ap, dims):
    return bass.AP(tensor=ap.tensor, offset=ap.offset, ap=[ap.ap[0]] + dims)


def can_wait(value):
    return not isinstance(value, int) or value > 0


def flamingo_gated_layer(nc, x, ctx_in, g_xattn, g_ffn, ssm_kernel, ssm_D, conv_w, Wq, Wk, Wv, Wg,
                         router_w, Wout, consts, out):
    NB, ROWS, L = x.shape
    HD = NB // 2
    NH = ROWS // HD
    CH = L // P
    RH, HDV, RATIO = router_w.shape
    DK = Wq.shape[1]
    HDK = DK // RH
    DV = Wv.shape[1]
    NROT = HD // 2
    PAIRS = RH // 2
    FULL = NROT * HD * NB
    HALF = HD // 2 * NB
    EXT = (HD + NROT) * NB
    ROW = HD * NB
    K0, LOG0 = DK, 2 * DK
    V0 = LOG0 + RH
    G0 = V0 + DV
    PROJ = G0 + DV

    xg = x.rearrange("b (h j) l -> h j b l", j=HD)
    cg = ctx_in.rearrange("b (h j) l -> h j b l", j=HD)
    og = out.rearrange("b (h j) l -> h j b l", j=HD)
    taps_dram = nc.dram_tensor("taps_dram", (NH, P + L), F32, kind="Internal")

    with ExitStack() as stack:
        def sb(name, *free):
            return stack.enter_context(nc.sbuf_tensor(name, [P, *free], F32))

        def parts(name, *free):
            return [stack.enter_context(nc.sbuf_tensor(f"{name}_{k}", [P, *free], F32R)) for k in ("high", "low")]

        def setup_sb(name, *free):
            return setup.enter_context(nc.sbuf_tensor(name, [P, *free], F32))

        def sem(name):
            return stack.enter_context(nc.semaphore(name))

        const = sb("const", C_COLS)
        w_all_p = parts("w_all", CH, PROJ)
        w_out_p = parts("w_out", CH, L)
        w_conv = sb("w_conv", CH, 2)
        gates = sb("gates", 2)
        d_tap = sb("d_tap", 1)
        w_mean = sb("w_mean", CH, RH)
        minus_half = sb("minus_half", RH)
        x_in = sb("x_in", 2, L)
        c_in = sb("c_in", 2, L)
        c_rev = sb("c_rev", CH, P)
        toep = sb("toep", L)
        held = sb("held", 1)
        stats1 = sb("stats1", 6)
        mv1 = sb("mv1", 2)
        ve1 = sb("ve1", 1)
        rstd1 = sb("rstd1", 1)
        qn = sb("qn", L)
        kx = sb("kx", CH, EXT)
        qx = sb("qx", 2, CH, EXT)
        kv = sb("kv", 2, FULL + HALF)
        kv_p = parts("kv", 2, CH, FULL + HALF)
        toep_p = parts("toep", 2, L)
        z_terms = sb("z_terms", CH, 8 * ROW)
        x2 = sb("x2", 2, L)
        stats2 = sb("stats2", 6)
        mv2 = sb("mv2", 2)
        ve2 = sb("ve2", 1)
        rstd2 = sb("rstd2", 1)
        z = sb("z", L)
        d_log = sb("d_log", RH)
        u = sb("u", RH)
        th = sb("th", RH)
        score = sb("score", RH)
        score1 = sb("score1", RH)
        cnt_a = sb("cnt_a", RH)
        cnt = sb("cnt", RH)
        rcnt = sb("rcnt", RH)
        weight = sb("weight", RH)
        k_sel = sb("k_sel", RH, RATIO)
        q_sel = sb("q_sel", RH, RATIO)
        o_var = sb("o_var", RH)
        o_ve = sb("o_ve", RH)
        o_rstd = sb("o_rstd", RH)

        setup = ExitStack()
        w_all = setup_sb("w_all", CH, PROJ)
        w_out = setup_sb("w_out", CH, L)
        w_tmp = z_terms[:, :, 0:DV]
        router = setup_sb("router", RH * HDV, RATIO)
        router_d = setup_sb("router_d", RH * HDV)
        taps = setup_sb("taps", P + L)
        setup.close()
        y_raw = sb("y_raw", CH, P)
        qk_sb = sb("qk_sb", 2 * RH, HDK)
        rot_a = sb("rot_a", 2 * RH, HDK)
        rot_b = sb("rot_b", 2 * RH, HDK)
        v_sb = sb("v_sb", DV)
        gate_sb = sb("gate_sb", DV)
        qe = sb("qe", RH, RATIO * HDK)
        ke = sb("ke", RH, RATIO * HDK)
        qeT = sb("qeT", CH, P)
        keT = sb("keT", CH, P)
        att = sb("att", CH, CH, P)
        o_sq = sb("o_sq", RH, HDV)
        gated = sb("gated", DV)
        out_sb = sb("out_sb", 2, L)
        yT_p = parts("yT", CH, P)
        gatedT_p = parts("gatedT", CH, P)

        bank = [stack.enter_context(nc.psum_tensor(f"bank{i}", [P, 512], F32)) for i in range(8)]

        ident = const[:, C_ID:C_ID + P]
        mask = const[:, C_MASK:C_MASK + P]
        causal = const[:, C_CAUSAL:C_CAUSAL + P]

        s_taps_in, s_taps_out, s_consts, s_gates, s_wv, s_weights, s_wout = (
            sem(n) for n in ("s_taps_in", "s_taps_out", "s_consts", "s_gates", "s_wv", "s_weights", "s_wout"))
        s_x = [sem(f"s_x{i}") for i in range(2)]
        s_c = [sem(f"s_c{i}") for i in range(2)]
        s_toep = [sem(f"s_toep{i}") for i in range(2)]
        s_stored = [sem(f"s_stored{i}") for i in range(2)]
        taps_zero, taps_ready, gates_ready, wout_ready = (
            sem("taps_zero"), sem("taps_ready"), sem("gates_ready"), sem("wout_ready"))
        w_step, w_centred, w_high, w_ready, half_ready = (
            sem("w_step"), sem("w_centred"), sem("w_high"), sem("w_ready"), sem("half_ready"))
        conv_last_ps = sem("conv_last_ps")
        gatedT_ps, zT_ps, out_ps, logit_ps, q_ps, v_ps, g_ps, cnt_ps = (
            sem(n) for n in ("gatedT_ps", "zT_ps", "out_ps", "logit_ps", "q_ps", "v_ps", "g_ps", "cnt_ps"))
        conv_ps = [sem(f"conv_ps{i}") for i in range(CH)]
        qeT_ps, keT_ps, cT_ps, qT_ps, xo_ps, o_ps = (
            sem(n) for n in ("qeT_ps", "keT_ps", "cT_ps", "qT_ps", "xo_ps", "o_ps"))
        attn_ps = [sem(f"attn_ps{i}") for i in range(2)]
        gatedT_high, y_cur, y_ready, th_ready, qk_copied, v_copied, gate_ready = (
            sem(n) for n in ("gatedT_high", "y_cur", "y_ready", "th_ready", "qk_copied", "v_copied", "gate_ready"))
        qeT_sb, keT_sb, kx_ready, qx_ready, o_squared = (
            sem(n) for n in ("qeT_sb", "keT_sb", "kx_ready", "qx_ready", "o_squared"))
        crev_ready = sem("crev_ready")
        y_high, toep_high = sem("y_high"), sem("toep_high")
        kv_high = [sem(f"kv_high{i}") for i in range(CH)]
        toep_ready = sem("toep_ready")
        kv_made = [sem(f"kv_made{i}") for i in range(CH)]
        sum_done = [sem(f"sum_done{i}") for i in range(CH - 1)]
        rot_prod, rot_ready, rstd1_ready, rstd2_ready, o_rstd_ready = (
            sem(n) for n in ("rot_prod", "rot_ready", "rstd1_ready", "rstd2_ready", "o_rstd_ready"))
        kv_ready = [sem(f"kv_ready{i}") for i in range(CH)]
        mul_done = [sem(f"mul_done{i}") for i in range(CH)]
        mask_done = [sem(f"mask_done{i}") for i in range(CH)]
        y_low, gatedT_ready, sum_last = sem("y_low"), sem("gatedT_ready"), sem("sum_last")
        sum_step, sum_pair, sums_ready = sem("sum_step"), sem("sum_pair"), sem("sums_ready")
        (mul_last, y_conv, out_ready, d_ready, u_ready, ksel_ready, route_a, route_b, route_c, qsel_ready,
         ke_ready, qe_ready, bn1_done, mv1_done, ve1_ready, qn_ready, x2_ready, bn2_done, mv2_done,
         ve2_ready, z_ready, o_summed, o_ve_ready, o_normed, gated_ready) = (
            sem(n) for n in ("mul_last", "y_conv", "out_ready", "d_ready", "u_ready", "ksel_ready", "route_a",
                             "route_b", "route_c", "qsel_ready", "ke_ready", "qe_ready", "bn1_done",
                             "mv1_done", "ve1_ready", "qn_ready", "x2_ready", "bn2_done", "mv2_done", "ve2_ready",
                             "z_ready", "o_summed", "o_ve_ready", "o_normed", "gated_ready"))

        FIRST, LAST = -2, NH
        LOOP = (2, NH // 2 - 2)

        def run(eng, step):
            def peeled(h):
                step(h // 2, h % 2, 0 <= h - 1, 0 <= h < NH, 0 <= h + 1 < NH, h + 2 < NH)
            for h in range(FIRST, 2 * LOOP[0]):
                peeled(h)
            with eng.Fori(*LOOP) as t:
                for p in range(2):
                    step(t, p, True, True, True, True)
            for h in range(2 * LOOP[1], LAST + 1):
                peeled(h)

        SCORE_BANKS = (0, 7, 5, 3)
        PASSES = ((0, 0), (0, 1), (1, 0))

        block = stack.enter_context(nc.Block())

        @block.sync
        def _(eng):
            eng.dma_start(c_in[:, 0, :], cg[0]).then_inc(s_c[0], 16)
            eng.dma_start(const[:, :], consts).then_inc(s_consts, 16)
            eng.dma_start(taps[0:NH, P:P + L], ssm_kernel).then_inc(s_taps_in, 16)
            eng.dma_start(d_tap[0:NH, :], ssm_D.rearrange("(h a) -> h a", a=1)).then_inc(s_taps_in, 16)
            eng.dma_start(x_in[:, 0, :], xg[0]).then_inc(s_x[0], 16)
            eng.wait_ge(taps_ready, 1)
            eng.dma_start(taps_dram.ap(), taps[0:NH, :]).then_inc(s_taps_out, 16)
            eng.dma_start(c_in[:, 1, :], cg[1]).then_inc(s_c[1], 16)
            eng.wait_ge(s_taps_out, 16)

            def toeplitz(t, p, h):
                src = taps_dram.ap()[h, :]
                src = bass.AP(tensor=src.tensor, offset=src.offset + 1, ap=[[1, P], [1, L]])
                eng.dma_start(toep[:, :], src).then_inc(s_toep[p], 16)

            def step(t, p, tail, back, front, pre):
                h = 2 * t + p
                if pre:
                    if not (isinstance(h, int) and h < -1):
                        if can_wait(h + 1):
                            eng.wait_ge(x2_ready, h + 1)
                        eng.dma_start(x_in[:, p, :], xg[h + 2]).then_inc(s_x[p], 16)
                    if can_wait(h + 2):
                        eng.wait_ge(toep_ready, h + 2)
                    toeplitz(t + 1, p, h + 2)
                if not isinstance(h, int) or -1 <= h < NH - 3:
                    if can_wait(h + 2):
                        eng.wait_ge(crev_ready, h + 2)
                    eng.dma_start(c_in[:, 1 - p, :], cg[h + 3]).then_inc(s_c[1 - p], 16)
                if tail:
                    eng.wait_ge(out_ready, h)
                    eng.dma_start(og[h - 1], out_sb[:, 1 - p, :]).then_inc(s_stored[1 - p], 16)

            run(eng, step)
            for p in range(2):
                eng.wait_ge(s_stored[p], 16 * (NH // 2))

        @block.tensor
        def _(eng):
            def transpose4(dst, src, last):
                for c in range(CH):
                    ins = nc.tensor.transpose(dst[:, c * P:(c + 1) * P], src(c), ident)
                ins.then_inc(last, 1)

            def conv(p, lc, h1, between=None, n=0):
                for mc in range(lc + 1):
                    if lc == mc:
                        eng.wait_ge(kv_ready[mc], h1 + 1)
                    for i, (a, b) in enumerate(PASSES):
                        ins = nc.tensor.matmul(bank[lc % 2][:, :], toep_p[a][:, 1 - p, (lc - mc) * P:(lc - mc + 1) * P],
                                               kv_p[b][:, 1 - p, mc, 0:FULL],
                                               start=(mc == 0 and i == 0), stop=(mc == lc and i == len(PASSES) - 1))
                        if mc == lc and i == len(PASSES) - 1:
                            ins.then_inc(conv_ps[lc], 1)
                        if between is not None:
                            between(n)
                            n += 1

            def conv_last(p, h1):
                eng.wait_ge(kv_ready[CH - 1], h1 + 1)
                for diag in range(CH):
                    for i, (a, b) in enumerate(PASSES):
                        ins = nc.tensor.matmul(bank[2][:, diag * HALF:CH * HALF], toep_p[a][:, 1 - p, diag * P:(diag + 1) * P],
                                               kv_p[b][:, 1 - p, 0:CH - diag, FULL:FULL + HALF],
                                               start=(diag == 0 and i == 0), stop=(diag == CH - 1 and i == len(PASSES) - 1),
                                               skip_group_check=True)
                ins.then_inc(conv_last_ps, 1)

            def project(dst, src_p, w_p, c0, cols, done, low_ready, value, between=None, passes=range(len(PASSES))):
                for i in passes:
                    a, b = PASSES[i]
                    if a == 1:
                        eng.wait_ge(low_ready, value)
                    for c in range(CH):
                        ins = nc.tensor.matmul(dst[:, 0:cols], src_p[a][:, c, :], w_p[b][:, c, c0:c0 + cols],
                                               start=(i == 0 and c == 0), stop=(i == len(PASSES) - 1 and c == CH - 1))
                        if i == len(PASSES) - 1 and c == CH - 1:
                            ins.then_inc(done, 1)
                        if between is not None and i > 0:
                            between((i - 1) * CH + c)

            eng.wait_ge(s_consts, 16)

            def step(t, p, tail, back, front, pre):
                h = 2 * t + p

                def attention_output(n):
                    if n == 0:
                        eng.wait_ge(v_copied, h)
                    if n < PAIRS:
                        for k in (2 * n, 2 * n + 1):
                            r, c = k // CH, k % CH
                            if c == 0:
                                eng.wait_ge(mask_done[r], h)
                            i = CH * c + r
                            ins = nc.tensor.matmul(bank[4][:, i * HDV:(i + 1) * HDV], att[:, r, c, :],
                                                   v_sb[:, i * HDV:(i + 1) * HDV], start=True, stop=True)
                        if n == PAIRS - 1:
                            ins.then_inc(o_ps, 1)

                def scores(n):
                    if n == 0:
                        if tail:
                            eng.wait_ge(gatedT_ready, h)
                        eng.wait_ge(keT_sb, h + 1)
                        eng.wait_ge(qeT_sb, h + 1)
                        if front:
                            eng.wait_ge(mul_done[2], h + 2)
                        elif can_wait(h):
                            eng.wait_ge(mask_done[0], h)
                    half, c = n // CH, n % CH
                    for r in (2 * half, 2 * half + 1):
                        rows = slice(r * 32, r * 32 + 32)
                        ins = nc.tensor.matmul(bank[SCORE_BANKS[r]][:, c * P:(c + 1) * P], keT[rows, c, :],
                                               qeT[rows, c, :], start=True, stop=True)
                    if c == CH - 1:
                        ins.then_inc(attn_ps[half], 1)

                def transpose_ctx():
                    eng.wait_ge(crev_ready, h + 3)
                    if can_wait(h):
                        eng.wait_ge(mask_done[3], h)
                    elif can_wait(h + 2):
                        eng.wait_ge(kx_ready, h + 2)
                    transpose4(bank[3], lambda c: c_rev[:, c, :], cT_ps)

                woven = front and tail and not (isinstance(h, int) and h == 1)
                if pre and not back:
                    transpose_ctx()
                if front:
                    eng.wait_ge(toep_ready, h + 2)
                    if can_wait(h):
                        eng.wait_ge(mask_done[0], h)
                    conv(p, 0, h + 1, attention_output if woven else None)
                    if can_wait(h + 1):
                        eng.wait_ge(mul_done[3], h + 1)
                    conv(p, 1, h + 1, attention_output if woven else None, len(PASSES))
                if tail and not woven:
                    for n in range(PAIRS):
                        attention_output(n)
                if back:
                    eng.wait_ge(z_ready, h + 1)
                    if can_wait(h):
                        eng.wait_ge(mask_done[1], h)
                    transpose4(bank[7], lambda c: z[:, c * P:(c + 1) * P], zT_ps)
                if pre and back:
                    transpose_ctx()
                if front:
                    eng.wait_ge(mul_done[0], h + 2)
                    conv(p, 2, h + 1)
                    if can_wait(h + 1):
                        eng.wait_ge(x2_ready, h + 1)
                    conv_last(p, h + 1)
                if back:
                    if isinstance(h, int) and h == 0:
                        eng.wait_ge(w_ready, CH)
                    eng.wait_ge(y_high, h + 1)
                    if pre:
                        eng.wait_ge(kx_ready, h + 3)
                    elif can_wait(h):
                        eng.wait_ge(mask_done[3], h)
                    project(bank[3], yT_p, w_all_p, 0, DK, q_ps, y_low, h + 1, passes=(0, 1))
                    if can_wait(h - 1):
                        eng.wait_ge(out_ready, h - 1)
                    project(bank[6], yT_p, w_all_p, K0, DK + RH, logit_ps, y_low, h + 1, passes=(0, 1))
                    project(bank[3], yT_p, w_all_p, 0, DK, q_ps, y_low, h + 1, passes=(2,))
                    project(bank[6], yT_p, w_all_p, K0, DK + RH, logit_ps, y_low, h + 1, passes=(2,))
                    if can_wait(h):
                        eng.wait_ge(o_normed, h)
                    project(bank[4], yT_p, w_all_p, V0, DV, v_ps, y_low, h + 1)
                if tail:
                    eng.wait_ge(gated_ready, h)
                    if back:
                        eng.wait_ge(y_conv, h + 1)
                    else:
                        eng.wait_ge(mask_done[1], h)
                    transpose4(bank[7], lambda c: gated[:, c * P:(c + 1) * P], gatedT_ps)
                if back:
                    eng.wait_ge(u_ready, h + 1)
                    eng.wait_ge(qk_copied, h + 1)
                    nc.tensor.matmul(bank[6][:, 0:RH], causal, u[:, :], start=True, stop=True).then_inc(cnt_ps, 1)
                    if can_wait(h):
                        eng.wait_ge(mask_done[2], h)
                    project(bank[5], yT_p, w_all_p, G0, DV, g_ps, y_low, h + 1)
                if pre:
                    eng.wait_ge(qn_ready, h + 3)
                    if front:
                        eng.wait_ge(mul_last, h + 2)
                    transpose4(bank[2], lambda c: qn[:, c * P:(c + 1) * P], qT_ps)
                if front:
                    eng.wait_ge(mul_done[1], h + 2)
                    conv(p, 3, h + 1)
                if back:
                    eng.wait_ge(ke_ready, h + 1)
                    eng.wait_ge(gate_ready, h + 1)
                    transpose4(bank[5], lambda c: ke[:, 4 * c:4 * c + 4, :], keT_ps)
                    eng.wait_ge(qe_ready, h + 1)
                    transpose4(bank[3], lambda c: qe[:, 4 * c:4 * c + 4, :], qeT_ps)
                if tail:
                    if isinstance(h, int) and h == 1:
                        eng.wait_ge(w_ready, CH + 1)
                    eng.wait_ge(gatedT_high, h)
                    if back:
                        eng.wait_ge(qsel_ready, h + 1)
                    else:
                        eng.wait_ge(out_ready, h - 1)
                    project(bank[6], gatedT_p, w_out_p, 0, L, out_ps, gatedT_ready, h,
                            scores if back else None)
                elif back:
                    for n in range(PAIRS):
                        scores(n)
                if front:
                    eng.wait_ge(sums_ready, 2 * h + 4)
                    if pre:
                        eng.wait_ge(qx_ready, h + 3)
                    transpose4(bank[2], lambda c: z_terms[:, c, 0:ROW], xo_ps)

            run(eng, step)

        @block.scalar
        def _(eng):
            eng.dma_start(gates[:, 0:1], g_xattn.rearrange("(a n) -> a n", a=1).partition_broadcast(P)
                          ).then_inc(s_gates, 16)
            eng.dma_start(gates[:, 1:2], g_ffn.rearrange("(a n) -> a n", a=1).partition_broadcast(P)
                          ).then_inc(s_gates, 16)
            eng.dma_start(w_conv[:, :, :], conv_w.rearrange("(c p) k -> p c k", p=P)).then_inc(s_gates, 16)
            eng.dma_start(router[:, :, :], router_w.rearrange("h v r -> (h v) r").partition_broadcast(P)
                          ).then_inc(s_wv, 16)
            eng.dma_start(w_all[:, :, V0:V0 + DV], Wv.rearrange("(c p) n -> p c n", p=P)).then_inc(s_wv, 16)

            def weights_high(c):
                if c == 0:
                    eng.wait_ge(s_weights, 48)
                    eng.wait_ge(w_centred, 1)
                eng.activation(w_all_p[0][:, c, :], w_all[:, c, :], ACT.Copy).then_inc(w_high, 1)

            def output_weights_high():
                eng.wait_ge(s_wout, 16)
                eng.wait_ge(gates_ready, 1)
                eng.activation(w_out[:, :, :], w_out[:, :, :], ACT.Copy, scale=gates[:, 1:2]).then_inc(wout_ready, 1)
                eng.wait_ge(wout_ready, 1)
                eng.activation(w_out_p[0][:, :, :], w_out[:, :, :], ACT.Copy).then_inc(w_high, 1)

            def extend(dst, src, done):
                psum = src[:, :].rearrange("p (c n) -> p c n", c=CH)
                eng.activation(dst[:, :, 0:ROW], psum, ACT.Copy)
                eng.activation(dst[:, :, ROW:EXT], psum[:, :, 0:EXT - ROW], ACT.Copy).then_inc(done, 1)

            def taps_high(t, p):
                eng.wait_ge(s_toep[p], 16 * (t + 2))
                eng.activation(toep_p[0][:, p, :], toep[:, :], ACT.Copy).then_inc(toep_high, 1)

            def kv_round(p, c, h2):
                eng.wait_ge(kv_made[c], h2 + 1)
                if can_wait(h2 - 1):
                    eng.wait_ge(conv_ps[CH - 1], h2 - 1)
                    eng.wait_ge(conv_last_ps, h2 - 1)
                eng.activation(kv_p[0][:, p, c, :], kv[:, c % 2, :], ACT.Copy).then_inc(kv_high[c], 1)

            def step(t, p, tail, back, front, pre):
                h = 2 * t + p
                first_step = isinstance(h, int) and h == -2
                setup_step = isinstance(h, int) and h == -1
                if pre:
                    eng.wait_ge(s_c[p], 16 * (t + 2))
                    if can_wait(h + 2):
                        eng.wait_ge(cT_ps, h + 2)
                    eng.activation(c_rev[:, :, :], view(c_in[:, p, P - 1:P], [[P, CH], [-1, P]]), ACT.Copy
                                   ).then_inc(crev_ready, 1)
                if setup_step:
                    weights_high(0)
                if tail:
                    eng.wait_ge(o_ps, h)
                    if can_wait(h - 1):
                        eng.wait_ge(o_summed, h - 1)
                    eng.activation(o_sq[:, :, :], bank[4][:, :].rearrange("p (a n) -> p a n", n=HDV), ACT.Square
                                   ).then_inc(o_squared, 1)
                if back:
                    eng.wait_ge(zT_ps, h + 1)
                    if can_wait(h):
                        eng.wait_ge(y_low, h)
                    elif isinstance(h, int):
                        eng.wait_ge(w_ready, CH)
                    for c in range(CH):
                        ins = eng.activation(y_raw[:, c, :], bank[7][:, c * P:(c + 1) * P], ACT.Copy,
                                             scale=w_conv[:, c, 1:2])
                    ins.then_inc(y_cur, 1)
                if pre:
                    eng.wait_ge(cT_ps, h + 3)
                    if can_wait(h + 2):
                        for c in range(CH):
                            eng.wait_ge(kv_made[c], h + 2)
                    extend(kx[:, :, :], bank[3], kx_ready)
                if first_step:
                    eng.wait_ge(s_gates, 48)
                    eng.activation(gates[:, :], gates[:, :], ACT.Tanh).then_inc(gates_ready, 1)
                if setup_step:
                    weights_high(1)
                    weights_high(2)
                if back:
                    eng.wait_ge(y_conv, h + 1)
                    if can_wait(h):
                        eng.wait_ge(g_ps, h)
                    eng.activation(yT_p[0][:, :, :], y_raw[:, :, :], ACT.Silu).then_inc(y_high, 1)
                if back:
                    eng.wait_ge(y_high, h + 1)
                    eng.activation(y_raw[:, :, :], y_raw[:, :, :], ACT.Silu).then_inc(y_ready, 1)
                if isinstance(h, int) and h == 0:
                    output_weights_high()
                if pre:
                    kv_round(p, 0, h + 2)
                if first_step:
                    taps_high(t, p)
                    for w, c0, cols in ((Wq, 0, DK), (Wk, K0, DK), (Wg, G0, DV)):
                        eng.dma_start(w_all[:, :, c0:c0 + cols], w.rearrange("(c p) n -> p c n", p=P)
                                      ).then_inc(s_weights, 16)
                    eng.dma_start(w_out[:, :, :], Wout.rearrange("(c p) n -> p c n", p=P)).then_inc(s_wout, 16)
                if setup_step:
                    weights_high(3)
                if back:
                    eng.wait_ge(q_ps, h + 1)
                    if can_wait(h):
                        eng.wait_ge(rot_prod, 3 * h)
                    eng.activation(qk_sb[:, 0:RH, :], bank[3][:, 0:DK].rearrange("p (a n) -> p a n", n=HDK),
                                   ACT.Silu)
                    eng.wait_ge(logit_ps, h + 1)
                    eng.activation(qk_sb[:, RH:2 * RH, :], bank[6][:, 0:DK].rearrange("p (a n) -> p a n", n=HDK),
                                   ACT.Copy).then_inc(qk_copied, 1)
                    eng.wait_ge(d_ready, h + 1)
                    if can_wait(h):
                        eng.wait_ge(route_a, h)
                    eng.activation(th[:, :], d_log[:, :], ACT.Tanh, scale=0.5).then_inc(th_ready, 1)
                if back:
                    eng.wait_ge(v_ps, h + 1)
                    if can_wait(h):
                        eng.wait_ge(o_ps, h)
                    eng.activation(v_sb[:, :], bank[4][:, :], ACT.Copy).then_inc(v_copied, 1)
                if tail:
                    eng.wait_ge(gatedT_ps, h)
                    if can_wait(h - 1):
                        eng.wait_ge(out_ps, h - 1)
                    eng.activation(gatedT_p[0][:, :, :], bank[7][:, :].rearrange("p (c n) -> p c n", c=CH), ACT.Copy
                                   ).then_inc(gatedT_high, 1)
                if pre:
                    kv_round(p, 1, h + 2)
                if back:
                    eng.wait_ge(g_ps, h + 1)
                    if can_wait(h):
                        eng.wait_ge(gated_ready, h)
                    eng.activation(gate_sb[:, :], bank[5][:, :], ACT.Silu).then_inc(gate_ready, 1)
                if pre:
                    eng.wait_ge(qT_ps, h + 3)
                    if can_wait(h + 1):
                        eng.wait_ge(mul_last, h + 1)
                        eng.wait_ge(mul_done[CH - 1], h + 1)
                    extend(qx[:, p, :, :], bank[2], qx_ready)
                if back:
                    eng.wait_ge(keT_ps, h + 1)
                    if can_wait(h):
                        eng.wait_ge(attn_ps[1], h)
                    eng.activation(keT[:, :, :], bank[5][:, :].rearrange("p (c n) -> p c n", c=CH), ACT.Copy
                                   ).then_inc(keT_sb, 1)
                    eng.wait_ge(qeT_ps, h + 1)
                    eng.activation(qeT[:, :, :], bank[3][:, :].rearrange("p (c n) -> p c n", c=CH), ACT.Copy
                                   ).then_inc(qeT_sb, 1)
                if pre:
                    kv_round(p, 2, h + 2)
                    if not first_step:
                        taps_high(t, p)
                if pre:
                    kv_round(p, 3, h + 2)

            run(eng, step)

        @block.gpsimd
        def _(eng):
            eng.memset(minus_half[:, :], -0.5).then_inc(half_ready, 1)
            eng.wait_ge(half_ready, 1)
            eng.wait_ge(s_consts, 16)

            def products(p, c, h2):
                if c == 0:
                    eng.wait_ge(kx_ready, h2 + 1)
                if c >= 2:
                    eng.wait_ge(kv_ready[c - 2], h2 + 1)
                elif can_wait(h2):
                    eng.wait_ge(kv_ready[c + 2], h2)
                eng.tensor_tensor(view(kv[:, c % 2, 0:FULL], [[ROW, NROT], [1, ROW]]),
                                  view(kx[:, c, 0:ROW], [[0, NROT], [1, ROW]]),
                                  view(kx[:, c, 0:ROW], [[NB, NROT], [1, ROW]]), ALU.mult)
                eng.tensor_tensor(kv[:, c % 2, FULL:FULL + HALF], kx[:, c, 0:HALF],
                                  kx[:, c, HALF:2 * HALF], ALU.mult).then_inc(kv_made[c], 1)

            def kv_rest(p, c, h2):
                eng.wait_ge(kv_high[c], h2 + 1)
                eng.tensor_tensor(kv_p[1][:, p, c, :], kv[:, c % 2, :], kv_p[0][:, p, c, :].bitcast(F32), ALU.subtract
                                  ).then_inc(kv_ready[c], 1)

            def taps_low(p, h2):
                eng.wait_ge(toep_high, h2 + 1)
                if can_wait(h2 - 1):
                    eng.wait_ge(conv_ps[CH - 1], h2 - 1)
                    eng.wait_ge(conv_last_ps, h2 - 1)
                eng.tensor_tensor(toep_p[1][:, p, :], toep[:, :], toep_p[0][:, p, :].bitcast(F32), ALU.subtract
                                  ).then_inc(toep_ready, 1)

            def add_terms(lc, h1):
                eng.wait_ge(mul_done[lc], h1 + 1)
                eng.tensor_tensor(z_terms[:, lc, 0:2 * ROW], z_terms[:, lc, 0:2 * ROW], z_terms[:, lc, 2 * ROW:4 * ROW],
                                  ALU.add).then_inc(sum_done[lc], 1)

            def rsqrt(dst, src, n, ready, value, done):
                eng.wait_ge(ready, value)
                eng.tensor_tensor(dst[:, 0:n], src[:, 0:n], minus_half[:, 0:n], ALU.pow).then_inc(done, 1)

            def step(t, p, tail, back, front, pre):
                h = 2 * t + p
                if tail:
                    rsqrt(o_rstd, o_ve, RH, o_ve_ready, h, o_rstd_ready)
                if pre:
                    products(p, 0, h + 2)
                if pre:
                    rsqrt(rstd1, ve1, 1, ve1_ready, h + 3, rstd1_ready)
                if front:
                    add_terms(0, h + 1)
                    add_terms(1, h + 1)
                if back:
                    eng.wait_ge(qk_copied, h + 1)
                    if can_wait(h):
                        eng.wait_ge(qe_ready, h)
                        eng.wait_ge(ke_ready, h)
                    eng.tensor_tensor(rot_a[:, :, :], qk_sb[:, :, :], view(const[:, C_COS:C_COS + 1], [[0, 2 * RH], [1, HDK]]),
                                      ALU.mult).then_inc(rot_prod, 1)
                    hf = HDK // 2
                    for a in range(2):
                        s = const[:, C_SIN + a * hf:C_SIN + a * hf + 1]
                        eng.tensor_tensor(rot_b[:, :, a * hf:(a + 1) * hf], qk_sb[:, :, (1 - a) * hf:(2 - a) * hf],
                                          view(s, [[0, 2 * RH], [1, hf]]), ALU.mult).then_inc(rot_prod, 1)
                    eng.wait_ge(rot_prod, 3 * h + 3)
                    eng.tensor_tensor(rot_a[:, :, :], rot_a[:, :, :], rot_b[:, :, :], ALU.add).then_inc(rot_ready, 1)
                if pre:
                    products(p, 1, h + 2)
                    kv_rest(p, 0, h + 2)
                    if not front:
                        taps_low(p, h + 2)
                if front:
                    add_terms(2, h + 1)
                if pre:
                    kv_rest(p, 1, h + 2)
                    products(p, 2, h + 2)
                    products(p, 3, h + 2)
                    kv_rest(p, 2, h + 2)
                    if front:
                        taps_low(p, h + 2)
                if pre:
                    kv_rest(p, 3, h + 2)
                if front:
                    rsqrt(rstd2, ve2, 1, ve2_ready, h + 2, rstd2_ready)

            run(eng, step)

        @block.vector
        def _(eng):
            eng.memset(taps[0:NH, 0:P], 0.0).then_inc(taps_zero, 1)
            eng.wait_ge(s_taps_in, 32)
            eng.tensor_tensor(taps[0:NH, P:P + 1], taps[0:NH, P:P + 1], d_tap[0:NH, :], ALU.add).then_inc(taps_zero, 1)
            eng.wait_ge(taps_zero, 2)
            eng.memset(u[:, :], 0.0).then_inc(taps_ready, 1)

            def prepare_weights():
                wv = w_all[:, :, V0:V0 + DV]
                eng.wait_ge(s_wv, 32)
                eng.tensor_tensor(router_d[:, :], router[:, :, 1], router[:, :, 0], ALU.subtract).then_inc(w_step, 1)
                eng.wait_ge(w_step, 1)
                eng.tensor_tensor(w_tmp, wv, view(router_d[:, 0:1], [[0, CH], [1, DV]]), ALU.mult
                                  ).then_inc(w_step, 1)
                eng.wait_ge(w_step, 2)
                for c in range(CH):
                    eng.tensor_reduce(w_all[:, c, LOG0:LOG0 + RH],
                                  w_tmp[:, c, :].rearrange("p (h v) -> p h v", v=HDV), AX_X, ALU.add
                                      ).then_inc(w_step, 1)
                for c in range(CH):
                    eng.tensor_reduce(w_mean[:, c, :], wv[:, c, :].rearrange("p (h v) -> p h v", v=HDV), AX_X, ALU.add
                                      ).then_inc(w_step, 1)
                eng.wait_ge(w_step, 2 + 2 * CH)
                eng.tensor_scalar(w_mean[:, :, :], w_mean[:, :, :], 1.0 / HDV, None, ALU.mult).then_inc(w_step, 1)
                eng.wait_ge(w_step, 3 + 2 * CH)
                for c in range(CH):
                    per_head = wv[:, c, :].rearrange("p (h v) -> p h v", v=HDV)
                    ins = eng.tensor_tensor(per_head, per_head, view(w_mean[:, c, 0:1], [[1, RH], [0, HDV]]), ALU.subtract)
                ins.then_inc(w_centred, 1)

            def weights_low(c):
                eng.wait_ge(w_high, c + 1)
                eng.tensor_tensor(w_all_p[1][:, c, :], w_all[:, c, :], w_all_p[0][:, c, :].bitcast(F32), ALU.subtract
                                  ).then_inc(w_ready, 1)

            def output_weights_low():
                eng.wait_ge(w_high, CH + 1)
                eng.tensor_tensor(w_out_p[1][:, :, :], w_out[:, :, :], w_out_p[0][:, :, :].bitcast(F32), ALU.subtract
                                  ).then_inc(w_ready, 1)

            def multiply(p, lc, h1):
                eng.wait_ge(conv_ps[lc], h1 + 1)
                if lc == 0:
                    eng.wait_ge(qx_ready, h1 + 1)
                    if can_wait(h1):
                        eng.wait_ge(xo_ps, h1)
                q = qx[:, 1 - p, lc, 0:1]
                y = bank[lc % 2]
                eng.tensor_tensor(view(z_terms[:, lc, 0:1], [[ROW, NROT], [1, ROW]]),
                                  view(y[:, 0:1], [[ROW, NROT], [1, ROW]]),
                                  view(q, [[NB, NROT], [1, ROW]]), ALU.mult)
                first = 4 * ROW + NB
                eng.tensor_tensor(view(z_terms[:, lc, first:first + 1], [[ROW + NB, NROT - 1], [1, ROW]]),
                                  view(y[:, ROW:ROW + 1], [[ROW, NROT - 1], [1, ROW]]),
                                  view(q, [[0, NROT - 1], [1, ROW]]), ALU.mult).then_inc(mul_done[lc], 1)

            def add_pairs(chunks, a, b, done):
                eng.tensor_tensor(z_terms[:, chunks, a * ROW:(a + 2) * ROW], z_terms[:, chunks, a * ROW:(a + 2) * ROW],
                                  z_terms[:, chunks, b * ROW:(b + 2) * ROW], ALU.add).then_inc(done, 1)

            def add_last(chunks):
                eng.tensor_tensor(z_terms[:, chunks, 0:ROW], z_terms[:, chunks, 0:ROW], z_terms[:, chunks, ROW:2 * ROW],
                                  ALU.add).then_inc(sums_ready, 1)

            def mask_scores(r):
                eng.tensor_tensor(att[:, r, :, :], bank[SCORE_BANKS[r]][:, :].rearrange("p (c n) -> p c n", c=CH),
                                  view(mask[:, 0:1], [[0, CH], [1, P]]), ALU.mult).then_inc(mask_done[r], 1)

            def expand(dst, at, sel, done):
                eng.tensor_tensor(view(dst[:, 0, 0:1], [[RATIO * HDK, RH], [HDK, RATIO], [1, HDK]]),
                                  view(rot_a[:, at, 0:1], [[HDK, RH], [0, RATIO], [1, HDK]]),
                                  view(sel[:, 0, 0:1], [[RATIO, RH], [1, RATIO], [0, HDK]]),
                                  ALU.mult).then_inc(done, 1)

            def multiply_last(p, h1):
                eng.wait_ge(conv_last_ps, h1 + 1)
                y = view(bank[2][:, 0:1], [[HALF, CH], [NB, 4], [1, NB]])
                q = qx[:, 1 - p, 0, :]
                a, b = 4 * ROW, 7 * ROW + HALF
                eng.tensor_tensor(view(z_terms[:, 0, a:a + 1], [[8 * ROW, CH], [ROW + NB, 4], [1, NB]]), y,
                                  view(q[:, HALF:HALF + 1], [[EXT, CH], [NB, 4], [1, NB]]), ALU.mult)
                eng.tensor_tensor(view(z_terms[:, 0, b:b + 1], [[8 * ROW, CH], [NB, 4], [1, NB]]), y,
                                  view(q[:, 0:1], [[EXT, CH], [NB, 4], [1, NB]]), ALU.mult).then_inc(mul_last, 1)

            def step(t, p, tail, back, front, pre):
                h = 2 * t + p
                setup_step = isinstance(h, int) and h == -1
                if front:
                    multiply(p, 0, h + 1)
                if tail:
                    eng.wait_ge(o_squared, h)
                    eng.tensor_reduce(o_var[:, :], o_sq[:, :, :], AX_X, ALU.add).then_inc(o_summed, 1)
                    eng.wait_ge(o_summed, h)
                    eng.tensor_scalar(o_ve[:, :], o_var[:, :], 1.0 / HDV, EPS, ALU.mult, ALU.add).then_inc(o_ve_ready, 1)
                if back:
                    eng.wait_ge(y_cur, h + 1)
                    for c in range(CH):
                        cur = y_raw[:, c, :].rearrange("p (j l) -> p j l", l=NB)[:, :, 1:NB]
                        prev = bank[7][:, c * P:(c + 1) * P].rearrange("p (j l) -> p j l", l=NB)[:, :, 0:NB - 1]
                        ins = eng.scalar_tensor_tensor(out=cur, in0=prev, scalar=w_conv[:, c, 0:1], in1=cur,
                                                       op0=ALU.mult, op1=ALU.add)
                    ins.then_inc(y_conv, 1)
                if front:
                    multiply(p, 1, h + 1)
                if setup_step:
                    weights_low(1)
                if back:
                    eng.wait_ge(y_high, h + 1)
                    eng.wait_ge(y_ready, h + 1)
                    eng.tensor_tensor(yT_p[1][:, :, :], y_raw[:, :, :], yT_p[0][:, :, :].bitcast(F32), ALU.subtract
                                      ).then_inc(y_low, 1)
                if pre:
                    eng.wait_ge(s_x[p], 16 * (t + 2))
                    eng.bn_stats(stats1[:, :], x_in[:, p, :]).then_inc(bn1_done, 1)
                    eng.wait_ge(bn1_done, h + 3)
                    eng.memset(held[:, :], 0.0)
                    eng.bn_aggr(mv1[:, :], stats1[:, :]).then_inc(mv1_done, 1)
                    eng.wait_ge(mv1_done, h + 3)
                    eng.tensor_scalar(ve1[:, :], mv1[:, 1:2], EPS, None, ALU.add).then_inc(ve1_ready, 1)
                if tail:
                    eng.wait_ge(o_rstd_ready, h)
                    if can_wait(h - 1):
                        eng.wait_ge(gatedT_ps, h - 1)
                    eng.tensor_tensor(gated[:, :].rearrange("p (a n) -> p a n", n=HDV),
                                      bank[4][:, :].rearrange("p (a n) -> p a n", n=HDV),
                                      view(o_rstd[:, 0:1], [[1, RH], [0, HDV]]), ALU.mult).then_inc(o_normed, 1)
                    eng.wait_ge(o_normed, h)
                    eng.wait_ge(gate_ready, h)
                    eng.tensor_tensor(gated[:, :], gated[:, :], gate_sb[:, :], ALU.mult).then_inc(gated_ready, 1)
                if front:
                    multiply(p, 2, h + 1)
                    multiply_last(p, h + 1)
                if back:
                    eng.wait_ge(logit_ps, h + 1)
                    if can_wait(h):
                        eng.wait_ge(th_ready, h)
                        eng.wait_ge(cnt_ps, h)
                    eng.wait_ge(qk_copied, h + 1)
                    eng.tensor_copy(d_log[:, :], bank[6][:, DK:DK + RH]).then_inc(d_ready, 1)
                    eng.wait_ge(d_ready, h + 1)
                    eng.tensor_scalar(u[:, :], d_log[:, :], 0.0, 0.5, ALU.is_gt, ALU.subtract).then_inc(u_ready, 1)
                    eng.tensor_scalar(k_sel[:, :, 0], d_log[:, :], 0.0, None, ALU.is_le)
                    eng.tensor_scalar(k_sel[:, :, 1], d_log[:, :], 0.0, None, ALU.is_gt).then_inc(ksel_ready, 1)
                    eng.wait_ge(th_ready, h + 1)
                    eng.wait_ge(u_ready, h + 1)
                    eng.tensor_tensor(score[:, :], th[:, :], u[:, :], ALU.mult).then_inc(route_a, 1)
                    eng.wait_ge(route_a, h + 1)
                    eng.tensor_scalar(score1[:, :], score[:, :], 0.5, None, ALU.add).then_inc(route_c, 1)
                if pre:
                    eng.wait_ge(rstd1_ready, h + 3)
                    if can_wait(h + 2):
                        eng.wait_ge(qT_ps, h + 2)
                    eng.tensor_scalar(qn[:, :], x_in[:, p, :], mv1[:, 0:1], rstd1[:, 0:1], ALU.subtract, ALU.mult
                                      ).then_inc(qn_ready, 1)
                if setup_step:
                    weights_low(2)
                if isinstance(h, int) and h == 0:
                    output_weights_low()
                if isinstance(h, int) and h == -2:
                    prepare_weights()
                    weights_low(0)
                if tail:
                    eng.wait_ge(gatedT_high, h)
                    eng.tensor_tensor(gatedT_p[1][:, :, :], bank[7][:, :].rearrange("p (c n) -> p c n", c=CH),
                                      gatedT_p[0][:, :, :].bitcast(F32), ALU.subtract).then_inc(gatedT_ready, 1)
                if back:
                    eng.wait_ge(rot_ready, h + 1)
                    eng.wait_ge(ksel_ready, h + 1)
                    if can_wait(h):
                        eng.wait_ge(keT_ps, h)
                        eng.wait_ge(qeT_ps, h)
                    expand(ke, RH, k_sel, ke_ready)
                if back:
                    eng.wait_ge(cnt_ps, h + 1)
                    eng.tensor_tensor(cnt_a[:, :], u[:, :], bank[6][:, 0:RH], ALU.mult).then_inc(route_b, 1)
                    eng.wait_ge(route_b, 4 * h + 1)
                    eng.tensor_scalar(cnt[:, :], cnt_a[:, :], 2.0, const[:, C_HALF:C_HALF + 1], ALU.mult, ALU.add
                                      ).then_inc(route_b, 1)
                    eng.wait_ge(route_b, 4 * h + 2)
                    eng.reciprocal(rcnt[:, :], cnt[:, :]).then_inc(route_b, 1)
                    eng.wait_ge(route_b, 4 * h + 3)
                    eng.wait_ge(route_c, h + 1)
                    eng.tensor_tensor(weight[:, :], score1[:, :], rcnt[:, :], ALU.mult).then_inc(route_b, 1)
                    eng.wait_ge(route_b, 4 * h + 4)
                    eng.tensor_tensor(q_sel[:, :, :], view(weight[:, 0:1], [[1, RH], [0, RATIO]]), k_sel[:, :, :],
                                      ALU.mult).then_inc(qsel_ready, 1)
                    eng.wait_ge(qsel_ready, h + 1)
                    expand(qe, 0, q_sel, qe_ready)
                if front:
                    eng.wait_ge(mul_last, h + 2)
                    eng.wait_ge(mul_done[CH - 2], h + 2)
                    add_pairs(slice(0, CH - 1), 4, 6, sum_step)
                    eng.wait_ge(sum_step, 2 * h + 3)
                    for c in range(CH - 1):
                        eng.wait_ge(sum_done[c], h + 2)
                    add_pairs(slice(0, CH - 1), 0, 4, sum_pair)
                    eng.wait_ge(sum_pair, 2 * h + 3)
                    add_last(slice(0, CH - 1))
                    multiply(p, 3, h + 1)
                    eng.wait_ge(mul_done[CH - 1], h + 2)
                    add_pairs(slice(CH - 1, CH), 0, 2, sum_last)
                    add_pairs(slice(CH - 1, CH), 4, 6, sum_step)
                    eng.wait_ge(sum_last, h + 2)
                    eng.wait_ge(sum_step, 2 * h + 4)
                    add_pairs(slice(CH - 1, CH), 0, 4, sum_pair)
                    eng.wait_ge(sum_pair, 2 * h + 4)
                    add_last(slice(CH - 1, CH))
                if setup_step:
                    weights_low(3)
                if isinstance(h, int) and h == 0:
                    eng.wait_ge(w_ready, CH + 1)
                if back:
                    eng.wait_ge(attn_ps[0], h + 1)
                    if can_wait(h):
                        eng.wait_ge(o_ps, h)
                    mask_scores(0)
                    mask_scores(1)
                    eng.wait_ge(attn_ps[1], h + 1)
                    mask_scores(2)
                if tail:
                    eng.wait_ge(out_ps, h)
                    if not isinstance(h, int) or h >= 3:
                        eng.wait_ge(s_stored[1 - p], 16 * (t + p - 1))
                    eng.tensor_tensor(out_sb[:, 1 - p, :], bank[6][:, :], x2[:, 1 - p, :], ALU.add
                                      ).then_inc(out_ready, 1)
                if back:
                    mask_scores(3)
                if front:
                    if tail:
                        eng.wait_ge(out_ready, h)
                    eng.wait_ge(xo_ps, h + 2)
                    if isinstance(h, int) and h == -1:
                        eng.wait_ge(gates_ready, 1)
                    eng.scalar_tensor_tensor(out=x2[:, 1 - p, :], in0=bank[2][:, :], scalar=gates[:, 0:1],
                                             in1=x_in[:, 1 - p, :], op0=ALU.mult, op1=ALU.add).then_inc(x2_ready, 1)
                    eng.wait_ge(x2_ready, h + 2)
                    eng.bn_stats(stats2[:, :], x2[:, 1 - p, :]).then_inc(bn2_done, 1)
                    eng.wait_ge(bn2_done, h + 2)
                    eng.memset(held[:, :], 0.0)
                    eng.bn_aggr(mv2[:, :], stats2[:, :]).then_inc(mv2_done, 1)
                    eng.wait_ge(mv2_done, h + 2)
                    eng.tensor_scalar(ve2[:, :], mv2[:, 1:2], EPS, None, ALU.add).then_inc(ve2_ready, 1)
                    eng.wait_ge(rstd2_ready, h + 2)
                    if can_wait(h + 1):
                        eng.wait_ge(zT_ps, h + 1)
                    eng.tensor_scalar(z[:, :], x2[:, 1 - p, :], mv2[:, 0:1], rstd2[:, 0:1], ALU.subtract, ALU.mult
                                      ).then_inc(z_ready, 1)

            run(eng, step)


def shape_constants(NB, HDK):
    p = np.arange(P)
    pos = p % NB
    same = (p[:, None] // NB == p[None, :] // NB) & (pos[:, None] <= pos[None, :])
    inv = (np.float32(1.0) / np.float32(10000.0) ** (np.arange(0, HDK, 2, dtype=np.float32) / np.float32(HDK)))
    f = pos[:, None].astype(np.float32) * inv[None, :].astype(np.float32)
    cos, sin = np.cos(f), np.sin(f)
    parts = [np.eye(P), same * HDK ** -0.5, same, cos, cos, -sin, sin, (pos[:, None] + 1) / 2]
    return np.concatenate([a.astype(np.float32) for a in parts], axis=1)


_NAMES = ["x", "ctx_2048", "g_xattn", "g_ffn", "L0_xattn_ssm_kernel", "L0_xattn_D", "L0_ffn_conv_w", "L0_ffn_Wq",
          "L0_ffn_Wk", "L0_ffn_Wv", "L0_ffn_Wg", "L0_ffn_router_w", "L0_ffn_Wout"]


def kernel(**inputs):
    import concourse.bacc as _bacc
    from concourse.bass_utils import run_bass_kernel_spmd as _run

    nc = _bacc.Bacc("TRN2", target_bir_lowering=False, num_devices=1)
    arrays, args = {}, []
    for name in _NAMES:
        a = np.ascontiguousarray(inputs[name])
        arrays[f"in_{name}"] = a
        args.append(nc.dram_tensor(f"in_{name}", a.shape, mybir.dt.from_np(a.dtype), kind="ExternalInput").ap())
    c = shape_constants(inputs["x"].shape[0], inputs["L0_ffn_Wq"].shape[1] // inputs["L0_ffn_router_w"].shape[0])
    arrays["shape_consts"] = c
    args.append(nc.dram_tensor("shape_consts", c.shape, F32, kind="ExternalInput").ap())
    args.append(nc.dram_tensor("out_x", inputs["x"].shape, F32, kind="ExternalOutput").ap())
    flamingo_gated_layer(nc, *args)
    r = _run(nc, [arrays], core_ids=[0])
    return r.results[0]["out_x"]
```
